# Optimizing a Trainium2 kernel written in Bass

```python
import numpy as np
import jax
import jax.numpy as jnp

def _softmax(x, axis=-1):
    return jax.nn.softmax(x, axis=axis)

def _gelu(x):
    return jax.nn.gelu(x, approximate=True)

def _silu(x):
    return jax.nn.silu(x)

def _sigmoid(x):
    return jax.nn.sigmoid(x)

def _layernorm(x, axis=-1, eps=1e-05):
    m = jnp.mean(x, axis=axis, keepdims=True)
    v = jnp.var(x, axis=axis, keepdims=True)
    return (x - m) / jnp.sqrt(v + eps)

def _scatter_add(tgt, idx, src, axis=0):
    return tgt.at[idx].add(src)

def _segment_sum(src, seg, n):
    return jax.ops.segment_sum(src, seg, n)
kernel_name = 'mk_flamingo_gated_d1_seqx_r8_652ce3'

def setup_inputs(seed: int=0):
    np.random.seed(seed)
    _w = jnp.asarray

    def _rec_inputs():
        import jax
        import jax.numpy as jnp
        _rk = jax.random.key(seed)
        x = -0.0003929 + 0.9999 * jax.random.normal(jax.random.fold_in(_rk, 1), (16, 256, 128), jnp.float32)
        _lenS = 256 - jax.random.randint(jax.random.fold_in(_rk, 7), (16,), 0, max(1, 256 // 4) + 1, jnp.int32)
        _lenS2 = 1601 - jax.random.randint(jax.random.fold_in(_rk, 8), (16,), 0, max(1, 1601 // 4) + 1, jnp.int32)
        _ctx_1024P = jax.random.normal(jax.random.fold_in(_rk, 11), (16, 16, 128), jnp.float32)
        _ctx_1024c = jax.random.dirichlet(jax.random.fold_in(_rk, 511), 0.3 * jnp.ones((16,), jnp.float32), (16, 1601))
        _ctx_1024t = jnp.einsum('bsk,bkd->bsd', _ctx_1024c, _ctx_1024P)
        _ctx_1024t = _ctx_1024t * jax.lax.rsqrt(jnp.mean(jnp.square(_ctx_1024t)) + 1e-12) * 0.953939
        ctx_1024 = 2.81802e-05 + 1.00001 * (_ctx_1024t + 0.3 * jax.random.normal(jax.random.fold_in(_rk, 611), (16, 1601, 128), jnp.float32))
        _g = jax.random.normal(jax.random.fold_in(_rk, 9001), (2, 1), jnp.float32)
        _g = jnp.sign(_g) * jnp.maximum(jnp.abs(_g), 1.0) + (_g == 0) * 1.0
        g_xattn = _g[0]
        g_ffn = _g[1]
        return (x, ctx_1024, g_xattn, g_ffn)
    x, ctx_1024, g_xattn, g_ffn = _rec_inputs()

    def _L0_xattn_setup():
        import jax, jax.numpy as jnp
        import numpy as np
        B, S, D = (8, 256, 128)
        EPS = 1e-05

        def _layernorm(x, w, b):
            mu = jnp.mean(x, axis=-1, keepdims=True)
            var = jnp.mean(jnp.square(x - mu), axis=-1, keepdims=True)
            return (x - mu) * jax.lax.rsqrt(var + EPS) * w + b
        key = jax.random.key(seed)
        ks = jax.random.split(key, 4)
        inp = {'query': jax.random.normal(ks[0], (B, S, D), jnp.float32), 'key': jax.random.normal(ks[1], (B, S, D), jnp.float32), 'value': jax.random.normal(ks[2], (B, S, D), jnp.float32), 'inv_scale_factor': jnp.full((1, 1), float(np.sqrt(D)), jnp.float32), 'dropout_p': 0}
        pk = jax.random.split(ks[3], 8)
        for i in range(1, 5):
            inp[f'ln{i}_w'] = 1.0 + 0.02 * jax.random.normal(pk[2 * (i - 1)], (D,), jnp.float32)
            inp[f'ln{i}_b'] = 0.02 * jax.random.normal(pk[2 * (i - 1) + 1], (D,), jnp.float32)
        return inp
    _L0_xattn_all = _L0_xattn_setup()
    _L0_xattn_in = {k: v for k, v in _L0_xattn_all.items() if k in ('inv_scale_factor', 'ln1_w', 'ln1_b', 'ln2_w', 'ln2_b', 'ln3_w', 'ln3_b', 'ln4_w', 'ln4_b')}
    del _L0_xattn_all

    def _L0_ffn_setup():
        import jax, jax.numpy as jnp
        import numpy as np
        DIM = 128

        def _reference_tuple_inner(x, W_r, W_k, W_v, mu_r, mu_k):
            B, T, C = x.shape
            x_prev = jnp.concatenate([jnp.zeros((B, 1, C), x.dtype), x[:, :-1, :]], axis=1)
            xr = mu_r * x + (1.0 - mu_r) * x_prev
            xk = mu_k * x + (1.0 - mu_k) * x_prev
            r = jax.nn.sigmoid(jnp.einsum('btc,dc->btd', xr, W_r))
            k = jnp.einsum('btc,dc->btd', xk, W_k)
            k_act = jnp.square(jax.nn.relu(k))
            out = r * jnp.einsum('btc,dc->btd', k_act, W_v)
            new_state = x[:, -1, :]
            return (out, new_state)
        key = jax.random.key(seed)
        ks = jax.random.split(key, 6)
        B, T, C = (8, 256, DIM)
        x = jax.random.normal(ks[0], (B, T, C), dtype=jnp.float32)
        s = 1.0 / np.sqrt(C)
        W_r = jax.random.uniform(ks[1], (C, C), jnp.float32, -s, s)
        W_k = jax.random.uniform(ks[2], (C, C), jnp.float32, -s, s)
        W_v = jax.random.uniform(ks[3], (C, C), jnp.float32, -s, s)
        mu_r = jax.random.uniform(ks[4], (C,), jnp.float32)
        mu_k = jax.random.uniform(ks[5], (C,), jnp.float32)
        return {'x': x, 'W_r': W_r, 'W_k': W_k, 'W_v': W_v, 'mu_r': mu_r, 'mu_k': mu_k}
    _L0_ffn_all = _L0_ffn_setup()
    _L0_ffn_in = {k: v for k, v in _L0_ffn_all.items() if k in ('W_r', 'W_k', 'W_v', 'mu_r', 'mu_k')}
    del _L0_ffn_all
    return {'x': x, 'ctx_1024': ctx_1024, 'g_xattn': g_xattn, 'g_ffn': g_ffn, 'L0_xattn_inv_scale_factor': _L0_xattn_in['inv_scale_factor'], 'L0_xattn_ln1_w': _L0_xattn_in['ln1_w'], 'L0_xattn_ln1_b': _L0_xattn_in['ln1_b'], 'L0_xattn_ln2_w': _L0_xattn_in['ln2_w'], 'L0_xattn_ln2_b': _L0_xattn_in['ln2_b'], 'L0_xattn_ln3_w': _L0_xattn_in['ln3_w'], 'L0_xattn_ln3_b': _L0_xattn_in['ln3_b'], 'L0_xattn_ln4_w': _L0_xattn_in['ln4_w'], 'L0_xattn_ln4_b': _L0_xattn_in['ln4_b'], 'L0_ffn_W_r': _L0_ffn_in['W_r'], 'L0_ffn_W_k': _L0_ffn_in['W_k'], 'L0_ffn_W_v': _L0_ffn_in['W_v'], 'L0_ffn_mu_r': _L0_ffn_in['mu_r'], 'L0_ffn_mu_k': _L0_ffn_in['mu_k']}

def reference(x, ctx_1024, g_xattn, g_ffn, L0_xattn_inv_scale_factor, L0_xattn_ln1_w, L0_xattn_ln1_b, L0_xattn_ln2_w, L0_xattn_ln2_b, L0_xattn_ln3_w, L0_xattn_ln3_b, L0_xattn_ln4_w, L0_xattn_ln4_b, L0_ffn_W_r, L0_ffn_W_k, L0_ffn_W_v, L0_ffn_mu_r, L0_ffn_mu_k):
    import jax
    import jax.numpy as jnp

    def _L0_xattn_ref(query, key, value, inv_scale_factor, ln1_w, ln1_b, ln2_w, ln2_b, ln3_w, ln3_b, ln4_w, ln4_b, dropout_p):
        import jax, jax.numpy as jnp
        import numpy as np
        B, S, D = (8, 256, 128)
        EPS = 1e-05

        def _layernorm(x, w, b):
            mu = jnp.mean(x, axis=-1, keepdims=True)
            var = jnp.mean(jnp.square(x - mu), axis=-1, keepdims=True)
            return (x - mu) * jax.lax.rsqrt(var + EPS) * w + b
        q = _layernorm(query, ln1_w, ln1_b)
        k = _layernorm(key, ln2_w, ln2_b)
        v = _layernorm(value, ln3_w, ln3_b)
        qk = jnp.einsum('bqd,bkd->bqk', q, k)
        scaled = qk / inv_scale_factor
        probs = jax.nn.softmax(scaled, axis=2)
        out = jnp.einsum('bqk,bkd->bqd', probs, v)
        return _layernorm(out, ln4_w, ln4_b)

    def _L0_ffn_ref(x, W_r, W_k, W_v, mu_r, mu_k):
        import jax, jax.numpy as jnp
        import numpy as np
        DIM = 128

        def _reference_tuple_inner(x, W_r, W_k, W_v, mu_r, mu_k):
            B, T, C = x.shape
            x_prev = jnp.concatenate([jnp.zeros((B, 1, C), x.dtype), x[:, :-1, :]], axis=1)
            xr = mu_r * x + (1.0 - mu_r) * x_prev
            xk = mu_k * x + (1.0 - mu_k) * x_prev
            r = jax.nn.sigmoid(jnp.einsum('btc,dc->btd', xr, W_r))
            k = jnp.einsum('btc,dc->btd', xk, W_k)
            k_act = jnp.square(jax.nn.relu(k))
            out = r * jnp.einsum('btc,dc->btd', k_act, W_v)
            new_state = x[:, -1, :]
            return (out, new_state)
        return _reference_tuple_inner(x, W_r, W_k, W_v, mu_r, mu_k)[0]
    x = x + jnp.tanh(g_xattn[0]) * _L0_xattn_ref(_layernorm(x, axis=-1), ctx_1024, ctx_1024, L0_xattn_inv_scale_factor, L0_xattn_ln1_w, L0_xattn_ln1_b, L0_xattn_ln2_w, L0_xattn_ln2_b, L0_xattn_ln3_w, L0_xattn_ln3_b, L0_xattn_ln4_w, L0_xattn_ln4_b, 0)
    x = x + jnp.tanh(g_ffn[0]) * _L0_ffn_ref(_layernorm(x, axis=-1), L0_ffn_W_r, L0_ffn_W_k, L0_ffn_W_v, L0_ffn_mu_r, L0_ffn_mu_k)
    return x

_drawn_inputs = setup_inputs


def setup_inputs(seed=0):
    import zlib

    import numpy as np

    out = dict(_drawn_inputs(seed))
    spreads = {}
    factors = {'L0_xattn_ln1_w': 8.0,
     'L0_xattn_ln1_b': 8.0,
     'L0_xattn_ln2_w': 8.0,
     'L0_xattn_ln2_b': 200.0,
     'L0_xattn_ln3_w': 13.22,
     'L0_xattn_ln4_w': 12.594,
     'L0_xattn_ln4_b': 36.523,
     'L0_ffn_W_r': 9.804,
     'L0_ffn_mu_r': 31.575,
     'L0_xattn_ln3_b': 37.597,
     'L0_ffn_mu_k': 3.631}
    for name, (base, spread) in spreads.items():
        noise = np.random.default_rng([zlib.crc32(name.encode()), seed]).standard_normal(out[name].shape)
        drawn = base * np.exp(spread * noise) if base else spread * noise
        out[name] = jnp.asarray(drawn.astype(out[name].dtype))
    for name, factor in factors.items():
        out[name] = (out[name] * factor).astype(out[name].dtype)
    return out
```

```python
import numpy as np
import concourse.bass as bass
from concourse import mybir
from contextlib import ExitStack

B, SQ, SK, D = 16, 256, 1601, 128
P = 128
QT = SQ // P
KT = -(-SK // P)
KF = SK // P
KR = SK - KF * P
GROUP = 4
NG = -(-KT // GROUP)
NW, BANK = 4, 512
WINDOW = -(-SK // NW)
REP = NW * WINDOW - SK
SC = NW * WINDOW + 1
EPS = 1e-5
LAG = 2
AHEAD = 2


class Batch:

    def __init__(self, n, half, parity, known):
        self.n, self.half, self.parity, self.known = n, half, parity, known

    def shift(self, k):
        q = self.parity + k
        return Batch(self.n + k, self.half + q // 2, q % 2, self.known)

    def exists(self):
        return not self.known or 0 <= self.n < B

    def upto(self, per_batch, done):
        return self.n * per_batch + done

    def loads(self, per_batch):
        return (self.half + 1) * per_batch


def run_pipeline(engine, iteration):
    first, last = LAG, B - AHEAD
    for n in range(-AHEAD, first):
        iteration(Batch(n, n // 2, n % 2, True))
    with engine.Fori(first // 2, last // 2) as half:
        for parity in range(2):
            iteration(Batch(half * 2 + parity, half, parity, False))
    for n in range(last, B + LAG):
        iteration(Batch(n, n // 2, n % 2, True))


def build(nc, x, ctx, g_xattn, g_ffn, inv_scale, w1, b1, w2, b2, w3, b3, w4, b4, W_r, W_k, W_v, mu_r, mu_k, out):
    f32, f32r = mybir.dt.float32, mybir.dt.float32r
    ALU, ACT, AX = mybir.AluOpType, mybir.ActivationFunctionType, mybir.AxisListType
    x_tiles = x.rearrange("b (t p) d -> b p t d", p=P)
    out_tiles = out.rearrange("b (t p) d -> b p t d", p=P)
    ctx_full = ctx[:, 0:KF * P, :].rearrange("b (p t) d -> b p t d", t=KF)
    ctx_rest = ctx[:, KF * P:SK, :]
    ctx_repeat = ctx[:, 0:REP, :]

    with ExitStack() as stack:
        def sb(name, shape, dt=f32):
            return stack.enter_context(nc.sbuf_tensor(name, shape, dt))

        def two(name, shape, dt=f32):
            return [sb(f"{name}{i}", shape, dt) for i in range(2)]

        def sem(name):
            return stack.enter_context(nc.semaphore(name))

        ident = sb("ident", [P, P])
        cols = sb("cols", [P, 16])
        W1, B1, W2, B2, MUR, MUK, INV, GX, GF = range(9)
        W1S, B1S, RINV, TGX, TGF, TGFH = range(9, 15)
        w_raw = sb("w_raw", [P, 3, D])
        w_t = sb("w_t", [P, 3, D])
        w3_bc, b3_bc = sb("w3_bc", [P, D]), sb("b3_bc", [P, D])
        w4_raw, b4_raw = sb("w4_raw", [P, D]), sb("b4_raw", [P, D])
        w4_bc, b4_bc = sb("w4_bc", [P, D]), sb("b4_bc", [P, D])
        minus_half = sb("minus_half", [P, 1])
        raw = two("raw", [P, KT, D])
        norm = two("norm", [P, KT, D])
        xq = two("xq", [P, QT, D])
        xres = two("xres", [P, QT, D])
        stats = two("stats", [P, KT + QT, 6])
        NS = KT + QT
        neg_mean = two("neg_mean", [P, NS])
        rstd = two("rstd", [P, NS])
        k_hi, k_lo = two("k_hi", [P, SC], f32r), two("k_lo", [P, SC], f32r)
        q_hi, q_lo = two("q_hi", [P, SQ], f32r), two("q_lo", [P, SQ], f32r)
        x1 = two("x1", [P, QT, D])
        result = two("result", [P, QT, D])
        z = sb("z", [P, QT, D])
        q_full = sb("q_full", [P, SQ])
        neg_s = two("neg_s", [P, NW * WINDOW])
        probs = two("probs", [P, SK])
        neg_max = sb("neg_max", [P, QT])
        sums = sb("sums", [P, QT])
        inv_sums = sb("inv_sums", [P, QT])
        pt = [sb(f"pt{g}", [P, GROUP * P]) for g in range(NG)]
        mix_a = sb("mix_a", [P, NS])
        mix_b = sb("mix_b", [P, NS])
        mix_c = sb("mix_c", [P, NS])
        mix_d = sb("mix_d", [P, NS])
        u = sb("u", [P, QT, D])
        o = sb("o", [P, QT, D])
        o3 = sb("o3", [P, QT, D])
        a4 = sb("a4", [P, QT, D])
        xb = sb("xb", [P, QT, D])
        st4, mv4, ve4, r4 = sb("st4", [P, QT, 6]), sb("mv4", [P, QT, 2]), sb("ve4", [P, QT]), sb("r4", [P, QT])
        st5, mv5, ve5, r5 = sb("st5", [P, QT, 6]), sb("mv5", [P, QT, 2]), sb("ve5", [P, QT]), sb("r5", [P, QT])
        y = sb("y", [P, QT, D])
        y_t = sb("y_t", [P, 1 + SQ])
        dy = sb("dy", [P, SQ])
        mixed_r, mixed_k = sb("mixed_r", [P, SQ]), sb("mixed_k", [P, SQ])
        gate = sb("gate", [P, QT, D])
        k_relu, k_sq = sb("k_relu", [P, SQ]), sb("k_sq", [P, SQ])
        gated = sb("gated", [P, QT, D])

        s_ps = stack.enter_context(nc.psum_tensor("s_ps", [P, NW * BANK], f32))
        t_ps = [stack.enter_context(nc.psum_tensor(f"t_ps{i}", [P, GROUP * P], f32)) for i in range(2)]
        z_ps = s_ps[:, (NW - 1) * BANK + P:(NW - 1) * BANK + P + SQ]
        u_ps = stack.enter_context(nc.psum_tensor("u_ps", [P, 512], f32))
        m_ps = stack.enter_context(nc.psum_tensor("m_ps", [P, 512], f32))

        consts_in = sem("consts_in")
        ident_set = sem("ident_set")
        pool_consts = sem("pool_consts")
        gates_set = sem("gates_set")
        dve_consts = sem("dve_consts")
        w_transposed = sem("w_transposed")
        w_copied = sem("w_copied")
        b2_high = sem("b2_high")
        ctx_in = [sem(f"ctx_in{i}") for i in range(2)]
        xq_in = [sem(f"xq_in{i}") for i in range(2)]
        xres_in = [sem(f"xres_in{i}") for i in range(2)]
        stored = [sem(f"stored{i}") for i in range(2)]
        stats_done = sem("stats_done")
        combined = sem("combined")
        rstd_done = sem("rstd_done")
        norm_done = sem("norm_done")
        z_done = sem("z_done")
        z_transposed = sem("z_transposed")
        q_evac = sem("q_evac")
        q_done = sem("q_done")
        k_transposed = sem("k_transposed")
        k_high = sem("k_high")
        k_done = sem("k_done")
        scores_done = sem("scores_done")
        max_done = sem("max_done")
        exp_done = sem("exp_done")
        sums_inv = sem("sums_inv")
        p_transposed = sem("p_transposed")
        p_evac = sem("p_evac")
        pv_done = sem("pv_done")
        u_done = sem("u_done")
        o_steps = sem("o_steps")
        xb_done = sem("xb_done")
        eps_added = sem("eps_added")
        ln_rstd = sem("ln_rstd")
        x1_steps = sem("x1_steps")
        y_done = sem("y_done")
        y_transposed = sem("y_transposed")
        y_evac = sem("y_evac")
        dy_done = sem("dy_done")
        mixed = sem("mixed")
        rk_done = sem("rk_done")
        gate_done = sem("gate_done")
        relu_done = sem("relu_done")
        k_squared = sem("k_squared")
        kv_done = sem("kv_done")
        gated_done = sem("gated_done")
        result_done = sem("result_done")
        pool_held = sem("pool_held")
        dve_held = sem("dve_held")

        N_CONSTS = 16
        block = stack.enter_context(nc.Block())

        def group_tiles(g):
            return range(g * GROUP, min((g + 1) * GROUP, KT))

        def rows(tile):
            return KR if tile == KT - 1 else P

        def rows_repeated(tile):
            return KR + REP if tile == KT - 1 else P

        def group_columns(g):
            lo = g * GROUP * P
            return lo, min(lo + GROUP * P, SC - 1)

        @block.sync
        def _(sp):
            def load_ctx(c):
                p = c.parity
                if not (c.known and c.n < 2):
                    sp.wait_ge(norm_done, c.shift(-2).upto(NG, NG))
                sp.dma_start(raw[p][:, 0:KF, :], ctx_full[c.n]).then_inc(ctx_in[p], 16)
                sp.dma_start(raw[p][0:KR, KF, :], ctx_rest[c.n]).then_inc(ctx_in[p], 16)
                sp.dma_start(raw[p][KR:KR + REP, KF, :], ctx_repeat[c.n]).then_inc(ctx_in[p], 16)

            def load_xq(c):
                if not (c.known and c.n < 2):
                    sp.wait_ge(z_done, c.shift(-2).upto(1, 1))
                sp.dma_start(xq[c.parity][:, :, :], x_tiles[c.n]).then_inc(xq_in[c.parity], 16)

            def load_xres(c):
                if not (c.known and c.n < 2):
                    sp.wait_ge(xb_done, c.shift(-2).upto(1, 1))
                sp.dma_start(xres[c.parity][:, :, :], x_tiles[c.n]).then_inc(xres_in[c.parity], 16)

            def store(c):
                sp.wait_ge(result_done, c.upto(1, 1))
                sp.dma_start(out_tiles[c.n], result[c.parity][:, :, :]).then_inc(stored[c.parity], 16)

            def iteration(b):
                if b.shift(2).exists():
                    load_xq(b.shift(2))
                    load_ctx(b.shift(2))
                if b.exists():
                    load_xres(b)
                if b.shift(-2).exists():
                    store(b.shift(-2))

            run_pipeline(sp, iteration)
            for p in range(2):
                sp.wait_ge(stored[p], 16 * (B // 2))

        @block.gpsimd
        def _(pool):
            nc.gpsimd.memset(ident[:, :], 0.0).then_inc(ident_set, 1)
            nc.gpsimd.memset(minus_half[:, :], -0.5).then_inc(pool_consts, 1)
            for p in range(2):
                nc.gpsimd.memset(stats[p][:, :, :], 1.0).then_inc(pool_consts, 1)
            nc.gpsimd.memset(y_t[:, 0:1], 0.0).then_inc(pool_consts, 1)
            pool.wait_ge(ident_set, 1)
            nc.gpsimd.affine_select(out=ident[:, :], in_=ident[:, :], compare_op=ALU.not_equal, fill=1.0, base=0,
                                    pattern=[[-1, P]], channel_multiplier=1).then_inc(ident_set, 1)
            pool.wait_ge(pool_consts, 4)

            def stand_alone():
                pool.sem_inc(pool_held, 1)

            def combine(c):
                st, xs = stats[c.parity], slice(KT, NS)
                mean_e, m2_e, mean_o, m2_o = st[:, :, 1], st[:, :, 2], st[:, :, 4], st[:, :, 5]
                steps = 6
                pool.wait_ge(stats_done, c.upto(1, 1))
                nc.gpsimd.tensor_tensor(mix_a[:, :], mean_e, mean_o, ALU.add)
                nc.gpsimd.tensor_tensor(mix_b[:, :], mean_e, mean_o, ALU.subtract)
                nc.gpsimd.tensor_tensor(mix_c[:, :], m2_e, m2_o, ALU.add).then_inc(combined, 1)
                pool.wait_ge(combined, c.upto(steps, 1))
                nc.gpsimd.tensor_tensor(mix_d[:, :], mix_b[:, :], mix_b[:, :], ALU.mult)
                nc.gpsimd.tensor_scalar(neg_mean[c.parity][:, :], mix_a[:, :], -0.5, 0.0, ALU.mult,
                                        ALU.add).then_inc(combined, 1)
                pool.wait_ge(combined, c.upto(steps, 2))
                stand_alone()
                nc.gpsimd.tensor_scalar(mix_b[:, :], mix_d[:, :], 0.25, 0.0, ALU.mult, ALU.add)
                nc.gpsimd.tensor_scalar(mix_a[:, :], mix_c[:, :], 1.0 / D, 0.0, ALU.mult, ALU.add).then_inc(combined, 1)
                pool.wait_ge(combined, c.upto(steps, 3))
                nc.gpsimd.tensor_tensor(mix_d[:, :], mix_a[:, :], mix_b[:, :], ALU.add).then_inc(combined, 1)
                pool.wait_ge(combined, c.upto(steps, 4))
                stand_alone()
                nc.gpsimd.tensor_scalar(mix_c[:, 0:KT], mix_d[:, 0:KT], 1.0, EPS, ALU.mult, ALU.add)
                nc.gpsimd.tensor_scalar(mix_c[:, xs], mix_d[:, xs], 1.0 + EPS, EPS * EPS, ALU.mult,
                                        ALU.add).then_inc(combined, 1)
                pool.wait_ge(combined, c.upto(steps, 5))
                nc.gpsimd.tensor_tensor(rstd[c.parity][:, :], mix_c[:, :], minus_half[:, :].broadcast_to([P, NS]),
                                        ALU.pow).then_inc(combined, 1)

            def normalise(c, g):
                p = c.parity
                if g == 0:
                    pool.wait_ge(combined, c.upto(6, 6))
                    if c.known and c.n < 2:
                        stand_alone()
                if not (c.known and c.n < 2):
                    pool.wait_ge(pv_done, c.shift(-2).upto(QT * NG, NG + g + 1))
                    stand_alone()
                for t in group_tiles(g):
                    r = rows_repeated(t)
                    last = nc.gpsimd.tensor_scalar(norm[p][0:r, t, :], raw[p][0:r, t, :], neg_mean[p][0:r, t:t + 1],
                                                   rstd[p][0:r, t:t + 1], ALU.add, ALU.mult)
                last.then_inc(norm_done, 1)

            def root(c, which, mv, ve, r, steps, step, per):
                pool.wait_ge(steps, c.upto(per, step))
                stand_alone()
                nc.gpsimd.tensor_scalar(ve[:, :], mv[:, :, 1], 1.0, EPS, ALU.mult, ALU.add).then_inc(eps_added, 1)
                pool.wait_ge(eps_added, c.upto(2, which + 1))
                nc.gpsimd.tensor_tensor(r[:, :], ve[:, :], minus_half[:, :].broadcast_to([P, QT]),
                                        ALU.pow).then_inc(ln_rstd, 1)

            def iteration(b):
                nxt, prev, old = b.shift(1), b.shift(-1), b.shift(-2)
                if nxt.exists():
                    combine(nxt)
                if old.exists():
                    pool.wait_ge(y_evac, old.upto(1, 1))
                    if not (old.known and old.n < 1):
                        pool.wait_ge(mixed, old.shift(-1).upto(1, 1))
                    nc.gpsimd.tensor_tensor(dy[:, :], y_t[:, 1:1 + SQ], y_t[:, 0:SQ], ALU.subtract).then_inc(dy_done, 1)
                if nxt.exists():
                    normalise(nxt, 0)
                    normalise(nxt, 1)
                if prev.exists():
                    if prev.known and prev.n == 0:
                        pool.wait_ge(dve_consts, 8)
                    pool.wait_ge(xres_in[prev.parity], prev.loads(16))
                    if not (prev.known and prev.n < 1):
                        pool.wait_ge(x1_steps, prev.shift(-1).upto(4, 2))
                    nc.gpsimd.tensor_tensor(xb[:, :, :], xres[prev.parity][:, :, :],
                                            b4_bc[:, :].unsqueeze(1).broadcast_to([P, QT, D]),
                                            ALU.add).then_inc(xb_done, 1)
                if nxt.exists():
                    normalise(nxt, 2)
                if prev.exists():
                    root(prev, 0, mv4, ve4, r4, o_steps, 4, 4)
                if nxt.exists():
                    normalise(nxt, 3)
                if prev.exists():
                    root(prev, 1, mv5, ve5, r5, x1_steps, 4, 4)

            run_pipeline(pool, iteration)

        @block.tensor
        def _(pe):
            pe.wait_ge(ident_set, 2)
            pe.wait_ge(consts_in, 16 * N_CONSTS)
            for i in range(3):
                last = nc.tensor.transpose(m_ps[:, i * D:(i + 1) * D], w_raw[:, i, :], ident[:, :])
            last.then_inc(w_transposed, 1)

            def scores(c, t):
                p = c.parity
                if t == 0:
                    pe.wait_ge(q_done, c.upto(1, 1))
                if not (c.known and c.n == 0 and t == 0):
                    pe.wait_ge(max_done, c.upto(QT, t))
                qs = slice(t * P, (t + 1) * P)
                for i in range(NW):
                    lo = i * WINDOW
                    ks = slice(lo, lo + WINDOW + 1)
                    if t == 0:
                        pe.wait_ge(k_done, c.upto(NG, min(-(-(lo + WINDOW + 1) // (GROUP * P)), NG)))
                    bank = s_ps[:, i * BANK:i * BANK + WINDOW + 1]
                    nc.tensor.matmul(bank, q_hi[p][:, qs], k_hi[p][:, ks], start=True, stop=False)
                    nc.tensor.matmul(bank, q_hi[p][:, qs], k_lo[p][:, ks], start=False, stop=False)
                    last = nc.tensor.matmul(bank, q_lo[p][:, qs], k_hi[p][:, ks], start=False, stop=True)
                last.then_inc(scores_done, 1)

            def transpose_probs(c, t, g):
                if g == 0:
                    pe.wait_ge(exp_done, c.upto(QT, t + 1))
                if not (c.known and c.n == 0 and t == 0 and g < 2):
                    pe.wait_ge(p_evac, c.upto(QT * NG, t * NG + g - 1))
                bank = t_ps[g % 2]
                for j, tile in enumerate(group_tiles(g)):
                    r = rows(tile)
                    last = nc.tensor.transpose(bank[0:r, j * P:(j + 1) * P], probs[t][:, tile * P:tile * P + r],
                                               ident[:, :])
                last.then_inc(p_transposed, 1)

            def pv(c, t, g):
                if g == 0 and not (c.known and c.n == 0 and t == 0):
                    pe.wait_ge(u_done, c.upto(QT, t))
                pe.wait_ge(p_evac, c.upto(QT * NG, t * NG + g + 1))
                for j, tile in enumerate(group_tiles(g)):
                    r = rows(tile)
                    last = nc.tensor.matmul(u_ps[:, 0:D], pt[g][0:r, j * P:(j + 1) * P], norm[c.parity][0:r, tile, :],
                                            start=(tile == 0), stop=(tile == KT - 1))
                last.then_inc(pv_done, 1)

            def transpose_keys(c, g):
                pe.wait_ge(norm_done, c.upto(NG, g + 1))
                if g == 0 and not (c.known and c.n == 0):
                    pe.wait_ge(max_done, c.shift(-1).upto(QT, QT))
                if g == NG - 1:
                    pe.wait_ge(q_evac, c.upto(2, 2))
                for j, tile in enumerate(group_tiles(g)):
                    r = rows_repeated(tile)
                    last = nc.tensor.transpose(s_ps[:, g * BANK + j * P:g * BANK + j * P + r], norm[c.parity][0:r, tile, :],
                                               ident[0:r, 0:r])
                last.then_inc(k_transposed, 1)

            def transpose_z(c):
                pe.wait_ge(z_done, c.upto(1, 1))
                if not (c.known and c.n == 0):
                    pe.wait_ge(max_done, c.shift(-1).upto(QT, QT))
                for t in range(QT):
                    last = nc.tensor.transpose(z_ps[:, t * P:(t + 1) * P], z[:, t, :], ident[:, :])
                last.then_inc(z_transposed, 1)

            def transpose_y(c):
                pe.wait_ge(y_done, c.upto(1, 1))
                if not (c.known and c.n == 0):
                    pe.wait_ge(gated_done, c.upto(1, 0))
                for t in range(QT):
                    last = nc.tensor.transpose(m_ps[:, t * P:(t + 1) * P], y[:, t, :], ident[:, :])
                last.then_inc(y_transposed, 1)

            def receptance_and_key(c):
                pe.wait_ge(mixed, c.upto(1, 1))
                for t in range(QT):
                    nc.tensor.matmul(m_ps[:, t * P:(t + 1) * P], mixed_r[:, t * P:(t + 1) * P], w_t[:, 0, :],
                                     start=True, stop=True)
                nc.tensor.matmul(m_ps[:, SQ:2 * SQ], w_t[:, 1, :], mixed_k[:, :], start=True,
                                 stop=True).then_inc(rk_done, 1)

            def value(c):
                pe.wait_ge(gate_done, c.upto(1, 1))
                pe.wait_ge(k_squared, c.upto(1, 1))
                for t in range(QT):
                    last = nc.tensor.matmul(m_ps[:, t * P:(t + 1) * P], k_sq[:, t * P:(t + 1) * P], w_t[:, 2, :],
                                            start=True, stop=True)
                last.then_inc(kv_done, 1)

            def iteration(b):
                nxt, prev, old = b.shift(1), b.shift(-1), b.shift(-2)
                if b.exists():
                    scores(b, 0)
                if old.exists():
                    transpose_y(old)
                if prev.exists():
                    transpose_probs(prev, 1, 0)
                    transpose_probs(prev, 1, 1)
                    pv(prev, 1, 0)
                    transpose_probs(prev, 1, 2)
                    transpose_probs(prev, 1, 3)
                    pv(prev, 1, 1)
                if old.exists():
                    receptance_and_key(old)
                if prev.exists():
                    pv(prev, 1, 2)
                    pv(prev, 1, 3)
                if b.exists():
                    scores(b, 1)
                    transpose_probs(b, 0, 0)
                    transpose_probs(b, 0, 1)
                if old.exists():
                    value(old)
                if b.exists():
                    pv(b, 0, 0)
                    transpose_probs(b, 0, 2)
                    transpose_probs(b, 0, 3)
                if nxt.exists():
                    transpose_z(nxt)
                    transpose_keys(nxt, 0)
                if b.exists():
                    pv(b, 0, 1)
                if nxt.exists():
                    transpose_keys(nxt, 1)
                if b.exists():
                    pv(b, 0, 2)
                if nxt.exists():
                    transpose_keys(nxt, 2)
                    transpose_keys(nxt, 3)
                if b.exists():
                    pv(b, 0, 3)

            pe.wait_ge(w_copied, 1)
            run_pipeline(pe, iteration)

        @block.scalar
        def _(act):
            def column(i):
                return cols[:, i:i + 1]

            for i, v in ((W1, w1), (B1, b1), (W2, w2), (B2, b2), (MUR, mu_r), (MUK, mu_k)):
                act.dma_start(column(i), v.rearrange("(d o) -> d o", o=1)).then_inc(consts_in, 16)
            act.dma_start(column(INV), inv_scale.broadcast_to([P, 1])).then_inc(consts_in, 16)
            act.dma_start(column(GX), g_xattn.rearrange("(a o) -> a o", o=1).broadcast_to([P, 1])).then_inc(consts_in, 16)
            act.dma_start(column(GF), g_ffn.rearrange("(a o) -> a o", o=1).broadcast_to([P, 1])).then_inc(consts_in, 16)
            for i, w in enumerate((W_r, W_k, W_v)):
                act.dma_start(w_raw[:, i, :], w).then_inc(consts_in, 16)
            for t, v in ((w3_bc, w3), (b3_bc, b3), (w4_raw, w4), (b4_raw, b4)):
                act.dma_start(t[:, :], v.rearrange("(o d) -> o d", o=1).broadcast_to([P, D])).then_inc(consts_in, 16)
            act.wait_ge(consts_in, 16 * N_CONSTS)
            nc.scalar.activation(cols[:, TGX:TGX + 2], cols[:, GX:GX + 2], ACT.Tanh).then_inc(gates_set, 1)
            for p in range(2):
                nc.scalar.activation(k_hi[p][:, SC - 1:SC], column(B2), ACT.Copy).then_inc(b2_high, 1)
            act.wait_ge(w_transposed, 1)
            nc.scalar.activation(w_t[:, :, :].rearrange("p a d -> p (a d)"), m_ps[:, 0:3 * D],
                                 ACT.Copy).then_inc(w_copied, 1)
            act.wait_ge(dve_consts, 8)

            def copy_probs(c, t, g):
                act.wait_ge(p_transposed, c.upto(QT * NG, t * NG + g + 1))
                if not (c.known and c.n == 0 and t == 0):
                    act.wait_ge(pv_done, c.upto(QT * NG, (t - 1) * NG + g + 1))
                tiles = group_tiles(g)
                r, n = rows(tiles[-1]), len(tiles) * P
                bank = t_ps[g % 2]
                nc.scalar.activation(pt[g][0:r, 0:n], bank[0:r, 0:n], ACT.Copy).then_inc(p_evac, 1)

            def exponentials(c, t):
                act.wait_ge(max_done, c.upto(QT, t + 1))
                if not (c.known and c.n == 0):
                    act.wait_ge(p_transposed, c.shift(-1).upto(QT * NG, (t + 1) * NG))
                    act.wait_ge(sums_inv, c.shift(-1).upto(QT, t + 1))
                nc.scalar.activation(probs[t][:, :], neg_s[t][:, 0:SK], ACT.Exp, bias=neg_max[:, t:t + 1], scale=-1.0,
                                     accum_out=sums[:, t:t + 1]).then_inc(exp_done, 1)

            def high_keys(c, g):
                act.wait_ge(k_transposed, c.upto(NG, g + 1))
                lo, hi = group_columns(g)
                nc.scalar.activation(k_hi[c.parity][:, lo:hi], s_ps[:, g * BANK:g * BANK + hi - lo], ACT.Copy,
                                     scale=column(W2)).then_inc(k_high, 1)

            def queries(c):
                act.wait_ge(z_transposed, c.upto(1, 1))
                if not (c.known and c.n == 0):
                    act.wait_ge(q_done, c.upto(1, 0))
                nc.scalar.activation(q_full[:, :], z_ps, ACT.Identity, bias=column(B1S),
                                     scale=column(W1S)).then_inc(q_evac, 1)
                nc.scalar.activation(q_hi[c.parity][:, :], z_ps, ACT.Identity, bias=column(B1S),
                                     scale=column(W1S)).then_inc(q_evac, 1)

            def attention_out(c, t):
                act.wait_ge(pv_done, c.upto(QT * NG, (t + 1) * NG))
                act.wait_ge(sums_inv, c.upto(QT, t + 1))
                if t == 0 and not (c.known and c.n == 0):
                    act.wait_ge(o_steps, c.upto(4, -3))
                nc.scalar.activation(u[:, t, :], u_ps[:, 0:D], ACT.Copy,
                                     scale=inv_sums[:, t:t + 1]).then_inc(u_done, 1)

            def copy_y(c):
                act.wait_ge(y_transposed, c.upto(1, 1))
                if not (c.known and c.n == 0):
                    act.wait_ge(mixed, c.upto(1, 0))
                nc.scalar.activation(y_t[:, 1:1 + SQ], m_ps[:, 0:SQ], ACT.Copy).then_inc(y_evac, 1)

            def gate_and_relu(c):
                act.wait_ge(rk_done, c.upto(1, 1))
                if not (c.known and c.n == 0):
                    act.wait_ge(gated_done, c.upto(1, 0))
                nc.scalar.activation(k_relu[:, :], m_ps[:, SQ:2 * SQ], ACT.Relu).then_inc(relu_done, 1)
                nc.scalar.activation(gate[:, :, :].rearrange("p t d -> p (t d)"), m_ps[:, 0:SQ], ACT.Tanh,
                                     scale=0.5).then_inc(gate_done, 1)
                act.wait_ge(relu_done, c.upto(1, 1))
                nc.scalar.activation(k_sq[:, :], k_relu[:, :], ACT.Square).then_inc(k_squared, 1)

            def iteration(b):
                nxt, prev, old = b.shift(1), b.shift(-1), b.shift(-2)
                if old.exists():
                    copy_y(old)
                if prev.exists():
                    copy_probs(prev, 1, 0)
                    copy_probs(prev, 1, 1)
                    copy_probs(prev, 1, 2)
                    copy_probs(prev, 1, 3)
                if b.exists():
                    exponentials(b, 0)
                if old.exists():
                    gate_and_relu(old)
                if prev.exists():
                    attention_out(prev, 1)
                if b.exists():
                    copy_probs(b, 0, 0)
                    copy_probs(b, 0, 1)
                    copy_probs(b, 0, 2)
                    copy_probs(b, 0, 3)
                if nxt.exists():
                    queries(nxt)
                    high_keys(nxt, 0)
                    high_keys(nxt, 1)
                if b.exists():
                    exponentials(b, 1)
                if nxt.exists():
                    high_keys(nxt, 2)
                    high_keys(nxt, 3)
                if b.exists():
                    attention_out(b, 0)

            run_pipeline(act, iteration)

        @block.vector
        def _(dve):
            def column(i):
                return cols[:, i:i + 1]

            dve.wait_ge(consts_in, 16 * N_CONSTS)
            nc.vector.reciprocal(column(RINV), column(INV)).then_inc(dve_consts, 1)
            dve.wait_ge(dve_consts, 1)
            nc.vector.tensor_scalar(column(W1S), column(W1), column(RINV), -1.0, ALU.mult, ALU.mult).then_inc(dve_consts, 1)
            nc.vector.tensor_scalar(column(B1S), column(B1), column(RINV), -1.0, ALU.mult, ALU.mult).then_inc(dve_consts, 1)
            dve.wait_ge(gates_set, 1)
            nc.vector.tensor_scalar(column(TGFH), column(TGF), 0.5, None, ALU.mult).then_inc(dve_consts, 1)
            nc.vector.tensor_scalar(w4_bc[:, :], w4_raw[:, :], column(TGX), None, ALU.mult).then_inc(dve_consts, 1)
            nc.vector.tensor_scalar(b4_bc[:, :], b4_raw[:, :], column(TGX), None, ALU.mult).then_inc(dve_consts, 1)
            dve.wait_ge(b2_high, 2)
            for p in range(2):
                nc.vector.tensor_tensor(k_lo[p][:, SC - 1:SC], column(B2), k_hi[p][:, SC - 1:SC].bitcast(f32),
                                        ALU.subtract).then_inc(dve_consts, 1)
            dve.wait_ge(dve_consts, 8)
            dve.wait_ge(pool_consts, 4)

            def statistics(c, tiles):
                p = c.parity
                if tiles[0] == 0:
                    dve.wait_ge(ctx_in[p], c.loads(48))
                    if not (c.known and c.n < 2):
                        dve.wait_ge(combined, c.shift(-2).upto(6, 6))
                for t in tiles:
                    r = rows_repeated(t)
                    nc.vector.bn_stats(stats[p][0:r, t, :], raw[p][0:r, t, :])
                if tiles[-1] == KT - 1:
                    dve.wait_ge(xq_in[p], c.loads(16))
                    for t in range(QT):
                        last = nc.vector.bn_stats(stats[p][:, KT + t, :], xq[p][:, t, :])
                    last.then_inc(stats_done, 1)

            def normalise_x(c):
                p = c.parity
                dve.wait_ge(combined, c.upto(6, 6))
                if not (c.known and c.n == 0):
                    dve.wait_ge(z_transposed, c.upto(1, 0))
                for t in range(QT):
                    last = nc.vector.tensor_scalar(z[:, t, :], xq[p][:, t, :], neg_mean[p][:, KT + t:KT + t + 1],
                                                   rstd[p][:, KT + t:KT + t + 1], ALU.add, ALU.mult)
                last.then_inc(z_done, 1)

            def low_queries(c):
                dve.wait_ge(q_evac, c.upto(2, 2))
                nc.vector.tensor_tensor(q_lo[c.parity][:, :], q_full[:, :], q_hi[c.parity][:, :].bitcast(f32),
                                        ALU.subtract).then_inc(q_done, 1)

            def low_keys(c, g):
                dve.wait_ge(k_high, c.upto(NG, g + 1))
                lo, hi = group_columns(g)
                nc.vector.scalar_tensor_tensor(k_lo[c.parity][:, lo:hi], s_ps[:, g * BANK:g * BANK + hi - lo], column(W2),
                                               k_hi[c.parity][:, lo:hi].bitcast(f32), ALU.mult,
                                               ALU.subtract).then_inc(k_done, 1)

            def maximum(c, t):
                dve.wait_ge(scores_done, c.upto(QT, t + 1))
                if not (c.known and c.n == 0):
                    dve.wait_ge(exp_done, c.shift(-1).upto(QT, t + 1))
                windows = s_ps[:, :].rearrange("p (w c) -> p w c", w=NW)[:, :, 0:WINDOW]
                q_b2 = s_ps[:, (NW - 1) * BANK + WINDOW:(NW - 1) * BANK + WINDOW + 1]
                joined = neg_s[t][:, :].rearrange("p (w c) -> p w c", w=NW)
                nc.vector.tensor_scalar(joined, windows, q_b2, None, ALU.add, ALU.min,
                                        accum_out=neg_max[:, t:t + 1]).then_inc(max_done, 1)

            def invert_sums(c, t):
                dve.wait_ge(exp_done, c.upto(QT, t + 1))
                if not (c.known and c.n == 0):
                    dve.wait_ge(u_done, c.shift(-1).upto(QT, t + 1))
                nc.vector.reciprocal(inv_sums[:, t:t + 1], sums[:, t:t + 1]).then_inc(sums_inv, 1)

            def value_affine(c):
                dve.wait_ge(u_done, c.upto(QT, QT))
                nc.vector.tensor_tensor(o3[:, :, :], u[:, :, :], w3_bc[:, :].unsqueeze(1).broadcast_to([P, QT, D]),
                                        ALU.mult).then_inc(o_steps, 1)
                dve.wait_ge(o_steps, c.upto(4, 1))
                nc.vector.tensor_tensor(o[:, :, :], o3[:, :, :], b3_bc[:, :].unsqueeze(1).broadcast_to([P, QT, D]),
                                        ALU.add).then_inc(o_steps, 1)
                dve.wait_ge(o_steps, c.upto(4, 2))
                for t in range(QT):
                    last = nc.vector.bn_stats(st4[:, t, :], o[:, t, :])
                last.then_inc(o_steps, 1)
                dve.wait_ge(o_steps, c.upto(4, 3))
                if not (c.known and c.n == 0):
                    dve.wait_ge(ln_rstd, c.upto(2, -1))
                dve.sem_inc(dve_held, 1)
                for t in range(QT):
                    last = nc.vector.bn_aggr(mv4[:, t, :], st4[:, t, :])
                last.then_inc(o_steps, 1)

            def residual(c):
                dve.wait_ge(o_steps, c.upto(4, 4))
                for t in range(QT):
                    last = nc.vector.scalar_tensor_tensor(a4[:, t, :], o[:, t, :], mv4[:, t, 0:1], w4_bc[:, :],
                                                          ALU.subtract, ALU.mult)
                last.then_inc(x1_steps, 1)
                dve.wait_ge(x1_steps, c.upto(4, 1))
                dve.wait_ge(ln_rstd, c.upto(2, 1))
                dve.wait_ge(xb_done, c.upto(1, 1))
                for t in range(QT):
                    last = nc.vector.scalar_tensor_tensor(x1[c.parity][:, t, :], a4[:, t, :], r4[:, t:t + 1],
                                                          xb[:, t, :], ALU.mult, ALU.add)
                last.then_inc(x1_steps, 1)
                dve.wait_ge(x1_steps, c.upto(4, 2))
                for t in range(QT):
                    last = nc.vector.bn_stats(st5[:, t, :], x1[c.parity][:, t, :])
                last.then_inc(x1_steps, 1)
                dve.wait_ge(x1_steps, c.upto(4, 3))
                dve.sem_inc(dve_held, 1)
                for t in range(QT):
                    last = nc.vector.bn_aggr(mv5[:, t, :], st5[:, t, :])
                last.then_inc(x1_steps, 1)

            def normalise_x1(c):
                dve.wait_ge(x1_steps, c.upto(4, 4))
                dve.wait_ge(ln_rstd, c.upto(2, 2))
                if not (c.known and c.n == 0):
                    dve.wait_ge(y_transposed, c.upto(1, 0))
                for t in range(QT):
                    last = nc.vector.tensor_scalar(y[:, t, :], x1[c.parity][:, t, :], mv5[:, t, 0:1], r5[:, t:t + 1],
                                                   ALU.subtract, ALU.mult)
                last.then_inc(y_done, 1)

            def mix(c):
                dve.wait_ge(dy_done, c.upto(1, 1))
                if not (c.known and c.n == 0):
                    dve.wait_ge(rk_done, c.upto(1, 0))
                nc.vector.scalar_tensor_tensor(mixed_r[:, :], dy[:, :], column(MUR), y_t[:, 0:SQ], ALU.mult, ALU.add)
                nc.vector.scalar_tensor_tensor(mixed_k[:, :], dy[:, :], column(MUK), y_t[:, 0:SQ], ALU.mult,
                                               ALU.add).then_inc(mixed, 1)

            def gated_value(c):
                dve.wait_ge(kv_done, c.upto(1, 1))
                if not (c.known and c.n < 2):
                    dve.wait_ge(stored[c.parity], c.shift(-2).loads(16))
                nc.vector.scalar_tensor_tensor(gated[:, :, :].rearrange("p t d -> p (t d)"),
                                               gate[:, :, :].rearrange("p t d -> p (t d)"), 1.0, m_ps[:, 0:SQ],
                                               ALU.add, ALU.mult).then_inc(gated_done, 1)
                dve.wait_ge(gated_done, c.upto(1, 1))
                nc.vector.scalar_tensor_tensor(result[c.parity][:, :, :], gated[:, :, :], column(TGFH),
                                               x1[c.parity][:, :, :], ALU.mult, ALU.add).then_inc(result_done, 1)

            def iteration(b):
                nxt, prev, old, new = b.shift(1), b.shift(-1), b.shift(-2), b.shift(2)
                if old.exists():
                    normalise_x1(old)
                if prev.exists():
                    invert_sums(prev, 1)
                if new.exists():
                    statistics(new, range(0, 6))
                if b.exists():
                    maximum(b, 0)
                if new.exists():
                    statistics(new, range(6, KT))
                if old.exists():
                    mix(old)
                if nxt.exists():
                    normalise_x(nxt)
                if b.exists():
                    invert_sums(b, 0)
                if prev.exists():
                    value_affine(prev)
                if b.exists():
                    maximum(b, 1)
                if old.exists():
                    gated_value(old)
                if prev.exists():
                    residual(prev)
                if nxt.exists():
                    low_queries(nxt)
                    for g in range(NG):
                        low_keys(nxt, g)

            run_pipeline(dve, iteration)


_INS = ["x", "ctx_1024", "g_xattn", "g_ffn", "L0_xattn_inv_scale_factor", "L0_xattn_ln1_w", "L0_xattn_ln1_b",
        "L0_xattn_ln2_w", "L0_xattn_ln2_b", "L0_xattn_ln3_w", "L0_xattn_ln3_b", "L0_xattn_ln4_w", "L0_xattn_ln4_b",
        "L0_ffn_W_r", "L0_ffn_W_k", "L0_ffn_W_v", "L0_ffn_mu_r", "L0_ffn_mu_k"]


def kernel(**inputs):
    import numpy as _np
    import concourse.bacc as _bacc
    from concourse import mybir as _mybir
    from concourse.bass_utils import run_bass_kernel_spmd as _run

    nc = _bacc.Bacc("TRN2", target_bir_lowering=False, num_devices=1)
    arrays, args = {}, []
    for name in _INS:
        a = _np.ascontiguousarray(inputs[name])
        arrays[f"in_{name}"] = a
        args.append(nc.dram_tensor(f"in_{name}", a.shape, _mybir.dt.from_np(a.dtype), kind="ExternalInput").ap())
    out = nc.dram_tensor("out_x", (B, SQ, D), _mybir.dt.float32, kind="ExternalOutput").ap()
    build(nc, *args, out)
    r = _run(nc, [arrays], core_ids=[0])
    return r.results[0]["out_x"]
```

```python
import numpy as np
import concourse.bass as bass
from concourse import mybir
from contextlib import ExitStack

B, SQ, SK, D = 16, 256, 1601, 128
P = 128
QT = SQ // P
KT = -(-SK // P)
KF = SK // P
KR = SK - KF * P
GROUP = 4
NG = -(-KT // GROUP)
HEAD = 2 * GROUP
NW, BANK = 4, 512
WINDOW = -(-SK // NW)
REP = NW * WINDOW - SK
SC = NW * WINDOW + 1
EPS = 1e-5
LAG = 2
AHEAD = 2


class Batch:

    def __init__(self, n, half, parity, known):
        self.n, self.half, self.parity, self.known = n, half, parity, known

    def shift(self, k):
        q = self.parity + k
        return Batch(self.n + k, self.half + q // 2, q % 2, self.known)

    def exists(self):
        return not self.known or 0 <= self.n < B

    def upto(self, per_batch, done):
        return self.n * per_batch + done

    def loads(self, per_batch):
        return (self.half + 1) * per_batch


def run_pipeline(engine, iteration):
    first, last = LAG, B - AHEAD
    for n in range(-AHEAD, first):
        iteration(Batch(n, n // 2, n % 2, True))
    with engine.Fori(first // 2, last // 2) as half:
        for parity in range(2):
            iteration(Batch(half * 2 + parity, half, parity, False))
    for n in range(last, B + LAG):
        iteration(Batch(n, n // 2, n % 2, True))


def build(nc, x, ctx, g_xattn, g_ffn, inv_scale, w1, b1, w2, b2, w3, b3, w4, b4, W_r, W_k, W_v, mu_r, mu_k, out):
    f32, f32r = mybir.dt.float32, mybir.dt.float32r
    ALU, ACT, AX = mybir.AluOpType, mybir.ActivationFunctionType, mybir.AxisListType
    x_tiles = x.rearrange("b (t p) d -> b p t d", p=P)
    out_tiles = out.rearrange("b (t p) d -> b p t d", p=P)
    ctx_full = ctx[:, 0:KF * P, :].rearrange("b (p t) d -> b p t d", t=KF)
    ctx_rest = ctx[:, KF * P:SK, :]
    ctx_repeat = ctx[:, 0:REP, :]

    with ExitStack() as stack:
        def sb(name, shape, dt=f32):
            return stack.enter_context(nc.sbuf_tensor(name, shape, dt))

        def two(name, shape, dt=f32):
            return [sb(f"{name}{i}", shape, dt) for i in range(2)]

        def sem(name):
            return stack.enter_context(nc.semaphore(name))

        ident = sb("ident", [P, P])
        cols = sb("cols", [P, 16])
        W1, B1, W2, B2, MUR, MUK, INV, GX, GF = range(9)
        W1S, B1S, RINV, TGX, TGF, TGFH = range(9, 15)
        w_raw = sb("w_raw", [P, 3, D])
        w_t = sb("w_t", [P, 3, D])
        w3_bc, b3_bc = sb("w3_bc", [P, D]), sb("b3_bc", [P, D])
        w4_raw, b4_raw = sb("w4_raw", [P, D]), sb("b4_raw", [P, D])
        w4_bc, b4_bc = sb("w4_bc", [P, D]), sb("b4_bc", [P, D])
        minus_half = sb("minus_half", [P, 1])
        raw = two("raw", [P, KT, D])
        norm = two("norm", [P, KT, D])
        xq = two("xq", [P, QT, D])
        xres = two("xres", [P, QT, D])
        stats = two("stats", [P, KT + QT, 6])
        NS = KT + QT
        neg_mean = two("neg_mean", [P, NS])
        rstd = two("rstd", [P, NS])
        k_hi, k_lo = two("k_hi", [P, SC], f32r), two("k_lo", [P, SC], f32r)
        q_hi, q_lo = two("q_hi", [P, SQ], f32r), two("q_lo", [P, SQ], f32r)
        x1 = two("x1", [P, QT, D])
        result = two("result", [P, QT, D])
        z = sb("z", [P, QT, D])
        q_full = sb("q_full", [P, SQ])
        neg_s = two("neg_s", [P, NW * WINDOW])
        probs = two("probs", [P, SK])
        neg_max = sb("neg_max", [P, QT])
        sums = sb("sums", [P, QT])
        inv_sums = sb("inv_sums", [P, QT])
        pt = [sb(f"pt{g}", [P, GROUP * P]) for g in range(NG)]
        mix_a = sb("mix_a", [P, NS])
        mix_b = sb("mix_b", [P, NS])
        mix_c = sb("mix_c", [P, NS])
        mix_d = sb("mix_d", [P, NS])
        u = sb("u", [P, QT, D])
        o = sb("o", [P, QT, D])
        o3 = sb("o3", [P, QT, D])
        a4 = sb("a4", [P, QT, D])
        xb = sb("xb", [P, QT, D])
        st4, mv4, ve4, r4 = sb("st4", [P, QT, 6]), sb("mv4", [P, QT, 2]), sb("ve4", [P, QT]), sb("r4", [P, QT])
        st5, mv5, ve5, r5 = sb("st5", [P, QT, 6]), sb("mv5", [P, QT, 2]), sb("ve5", [P, QT]), sb("r5", [P, QT])
        y = sb("y", [P, QT, D])
        y_t = sb("y_t", [P, 1 + SQ])
        dy = sb("dy", [P, SQ])
        mixed_r, mixed_k = sb("mixed_r", [P, SQ]), sb("mixed_k", [P, SQ])
        gate = sb("gate", [P, QT, D])
        k_relu, k_sq = sb("k_relu", [P, SQ]), sb("k_sq", [P, SQ])
        gated = sb("gated", [P, QT, D])

        s_ps = stack.enter_context(nc.psum_tensor("s_ps", [P, NW * BANK], f32))
        t_ps = [stack.enter_context(nc.psum_tensor(f"t_ps{i}", [P, GROUP * P], f32)) for i in range(2)]
        z_ps = s_ps[:, (NW - 1) * BANK + P:(NW - 1) * BANK + P + SQ]
        u_ps = stack.enter_context(nc.psum_tensor("u_ps", [P, 512], f32))
        m_ps = stack.enter_context(nc.psum_tensor("m_ps", [P, 512], f32))

        consts_in = sem("consts_in")
        weights_in = sem("weights_in")
        late_consts_in = sem("late_consts_in")
        ident_set = sem("ident_set")
        pool_consts = sem("pool_consts")
        gates_set = sem("gates_set")
        dve_consts = sem("dve_consts")
        w_transposed = sem("w_transposed")
        w_copied = sem("w_copied")
        b2_high = sem("b2_high")
        ctx_head_in = [sem(f"ctx_head_in{i}") for i in range(2)]
        ctx_tail_in = [sem(f"ctx_tail_in{i}") for i in range(2)]
        xq_in = [sem(f"xq_in{i}") for i in range(2)]
        xres_in = [sem(f"xres_in{i}") for i in range(2)]
        stored = [sem(f"stored{i}") for i in range(2)]
        stats_done = sem("stats_done")
        combined = sem("combined")
        rstd_done = sem("rstd_done")
        norm_done = sem("norm_done")
        z_done = sem("z_done")
        z_transposed = sem("z_transposed")
        q_evac = sem("q_evac")
        q_done = sem("q_done")
        k_transposed = sem("k_transposed")
        k_high = sem("k_high")
        k_done = sem("k_done")
        scores_done = sem("scores_done")
        max_done = sem("max_done")
        exp_done = sem("exp_done")
        sums_inv = sem("sums_inv")
        p_transposed = sem("p_transposed")
        p_evac = sem("p_evac")
        pv_done = sem("pv_done")
        u_done = sem("u_done")
        o_steps = sem("o_steps")
        xb_done = sem("xb_done")
        eps_added = sem("eps_added")
        ln_rstd = sem("ln_rstd")
        x1_steps = sem("x1_steps")
        y_done = sem("y_done")
        y_transposed = sem("y_transposed")
        y_evac = sem("y_evac")
        dy_done = sem("dy_done")
        mixed = sem("mixed")
        rk_done = sem("rk_done")
        gate_done = sem("gate_done")
        relu_done = sem("relu_done")
        k_squared = sem("k_squared")
        kv_done = sem("kv_done")
        gated_done = sem("gated_done")
        result_done = sem("result_done")
        pool_held = sem("pool_held")
        dve_held = sem("dve_held")

        N_CONSTS, N_WEIGHTS, N_LATE = 5, 3, 8
        block = stack.enter_context(nc.Block())

        def group_tiles(g):
            return range(g * GROUP, min((g + 1) * GROUP, KT))

        def rows(tile):
            return KR if tile == KT - 1 else P

        def rows_repeated(tile):
            return KR + REP if tile == KT - 1 else P

        def group_columns(g):
            lo = g * GROUP * P
            return lo, min(lo + GROUP * P, SC - 1)

        @block.sync
        def _(sp):
            def load_head(c):
                p = c.parity
                if not (c.known and c.n < 2):
                    sp.wait_ge(norm_done, c.shift(-2).upto(NG, 2))
                sp.dma_start(raw[p][:, 0:HEAD, :], ctx_full[c.n, :, 0:HEAD, :]).then_inc(ctx_head_in[p], 16)

            def load_tail(c):
                p = c.parity
                if not (c.known and c.n < 2):
                    sp.wait_ge(norm_done, c.shift(-2).upto(NG, NG))
                sp.dma_start(raw[p][:, HEAD:KF, :], ctx_full[c.n, :, HEAD:KF, :]).then_inc(ctx_tail_in[p], 16)
                sp.dma_start(raw[p][0:KR, KF, :], ctx_rest[c.n]).then_inc(ctx_tail_in[p], 16)
                sp.dma_start(raw[p][KR:KR + REP, KF, :], ctx_repeat[c.n]).then_inc(ctx_tail_in[p], 16)

            def load_xq(c):
                if not (c.known and c.n < 2):
                    sp.wait_ge(z_done, c.shift(-2).upto(1, 1))
                sp.dma_start(xq[c.parity][:, :, :], x_tiles[c.n]).then_inc(xq_in[c.parity], 16)

            def load_xres(c):
                if not (c.known and c.n < 2):
                    sp.wait_ge(xb_done, c.shift(-2).upto(1, 1))
                sp.dma_start(xres[c.parity][:, :, :], x_tiles[c.n]).then_inc(xres_in[c.parity], 16)

            def iteration(b):
                if b.shift(2).exists():
                    load_xq(b.shift(2))
                    load_head(b.shift(2))
                    load_tail(b.shift(2))
                if b.exists():
                    load_xres(b)

            run_pipeline(sp, iteration)
            for p in range(2):
                sp.wait_ge(stored[p], 16 * (B // 2))

        @block.gpsimd
        def _(pool):
            nc.gpsimd.memset(ident[:, :], 0.0).then_inc(ident_set, 1)
            nc.gpsimd.memset(minus_half[:, :], -0.5).then_inc(pool_consts, 1)
            for p in range(2):
                nc.gpsimd.memset(stats[p][:, :, :], 1.0).then_inc(pool_consts, 1)
            nc.gpsimd.memset(y_t[:, 0:1], 0.0).then_inc(pool_consts, 1)
            pool.wait_ge(ident_set, 1)
            nc.gpsimd.affine_select(out=ident[:, :], in_=ident[:, :], compare_op=ALU.not_equal, fill=1.0, base=0,
                                    pattern=[[-1, P]], channel_multiplier=1).then_inc(ident_set, 1)
            pool.wait_ge(pool_consts, 4)

            def stand_alone():
                pool.sem_inc(pool_held, 1)

            def combine(c):
                st, xs = stats[c.parity], slice(KT, NS)
                mean_e, m2_e, mean_o, m2_o = st[:, :, 1], st[:, :, 2], st[:, :, 4], st[:, :, 5]
                steps = 6
                pool.wait_ge(stats_done, c.upto(1, 1))
                nc.gpsimd.tensor_tensor(mix_a[:, :], mean_e, mean_o, ALU.add)
                nc.gpsimd.tensor_tensor(mix_b[:, :], mean_e, mean_o, ALU.subtract)
                nc.gpsimd.tensor_tensor(mix_c[:, :], m2_e, m2_o, ALU.add).then_inc(combined, 1)
                pool.wait_ge(combined, c.upto(steps, 1))
                nc.gpsimd.tensor_tensor(mix_d[:, :], mix_b[:, :], mix_b[:, :], ALU.mult)
                nc.gpsimd.tensor_scalar(neg_mean[c.parity][:, :], mix_a[:, :], -0.5, 0.0, ALU.mult,
                                        ALU.add).then_inc(combined, 1)
                pool.wait_ge(combined, c.upto(steps, 2))
                stand_alone()
                nc.gpsimd.tensor_scalar(mix_b[:, :], mix_d[:, :], 0.25, 0.0, ALU.mult, ALU.add)
                nc.gpsimd.tensor_scalar(mix_a[:, :], mix_c[:, :], 1.0 / D, 0.0, ALU.mult, ALU.add).then_inc(combined, 1)
                pool.wait_ge(combined, c.upto(steps, 3))
                nc.gpsimd.tensor_tensor(mix_d[:, :], mix_a[:, :], mix_b[:, :], ALU.add).then_inc(combined, 1)
                pool.wait_ge(combined, c.upto(steps, 4))
                stand_alone()
                nc.gpsimd.tensor_scalar(mix_c[:, 0:KT], mix_d[:, 0:KT], 1.0, EPS, ALU.mult, ALU.add)
                nc.gpsimd.tensor_scalar(mix_c[:, xs], mix_d[:, xs], 1.0 + EPS, EPS * EPS, ALU.mult,
                                        ALU.add).then_inc(combined, 1)
                pool.wait_ge(combined, c.upto(steps, 5))
                nc.gpsimd.tensor_tensor(rstd[c.parity][:, :], mix_c[:, :], minus_half[:, :].broadcast_to([P, NS]),
                                        ALU.pow).then_inc(combined, 1)

            def normalise(c, g):
                p = c.parity
                if g == 0:
                    pool.wait_ge(combined, c.upto(6, 6))
                    if c.known and c.n < 2:
                        stand_alone()
                if not (c.known and c.n < 2):
                    pool.wait_ge(pv_done, c.shift(-2).upto(QT * NG, NG + g + 1))
                    stand_alone()
                for t in group_tiles(g):
                    r = rows_repeated(t)
                    last = nc.gpsimd.tensor_scalar(norm[p][0:r, t, :], raw[p][0:r, t, :], neg_mean[p][0:r, t:t + 1],
                                                   rstd[p][0:r, t:t + 1], ALU.add, ALU.mult)
                last.then_inc(norm_done, 1)

            def root(c, which, mv, ve, r, steps, step, per):
                pool.wait_ge(steps, c.upto(per, step))
                stand_alone()
                nc.gpsimd.tensor_scalar(ve[:, :], mv[:, :, 1], 1.0, EPS, ALU.mult, ALU.add).then_inc(eps_added, 1)
                pool.wait_ge(eps_added, c.upto(2, which + 1))
                nc.gpsimd.tensor_tensor(r[:, :], ve[:, :], minus_half[:, :].broadcast_to([P, QT]),
                                        ALU.pow).then_inc(ln_rstd, 1)

            def iteration(b):
                nxt, prev = b.shift(1), b.shift(-1)
                if nxt.exists():
                    combine(nxt)
                if nxt.exists():
                    normalise(nxt, 0)
                    normalise(nxt, 1)
                if prev.exists():
                    if prev.known and prev.n == 0:
                        pool.wait_ge(dve_consts, 8)
                    pool.wait_ge(xres_in[prev.parity], prev.loads(16))
                    if not (prev.known and prev.n < 1):
                        pool.wait_ge(x1_steps, prev.shift(-1).upto(4, 2))
                    nc.gpsimd.tensor_tensor(xb[:, :, :], xres[prev.parity][:, :, :],
                                            b4_bc[:, :].unsqueeze(1).broadcast_to([P, QT, D]),
                                            ALU.add).then_inc(xb_done, 1)
                if nxt.exists():
                    normalise(nxt, 2)
                if prev.exists():
                    root(prev, 0, mv4, ve4, r4, o_steps, 4, 4)
                if nxt.exists():
                    normalise(nxt, 3)
                if prev.exists():
                    root(prev, 1, mv5, ve5, r5, x1_steps, 4, 4)

            run_pipeline(pool, iteration)

        @block.tensor
        def _(pe):
            pe.wait_ge(ident_set, 2)
            pe.wait_ge(weights_in, 16 * N_WEIGHTS)
            for i in range(3):
                last = nc.tensor.transpose(m_ps[:, i * D:(i + 1) * D], w_raw[:, i, :], ident[:, :])
            last.then_inc(w_transposed, 1)

            def scores(c, t):
                p = c.parity
                if t == 0:
                    pe.wait_ge(q_done, c.upto(1, 1))
                if not (c.known and c.n == 0 and t == 0):
                    pe.wait_ge(max_done, c.upto(QT, t))
                qs = slice(t * P, (t + 1) * P)
                for i in range(NW):
                    lo = i * WINDOW
                    ks = slice(lo, lo + WINDOW + 1)
                    if t == 0:
                        pe.wait_ge(k_done, c.upto(NG, min(-(-(lo + WINDOW + 1) // (GROUP * P)), NG)))
                    bank = s_ps[:, i * BANK:i * BANK + WINDOW + 1]
                    nc.tensor.matmul(bank, q_hi[p][:, qs], k_hi[p][:, ks], start=True, stop=False)
                    nc.tensor.matmul(bank, q_hi[p][:, qs], k_lo[p][:, ks], start=False, stop=False)
                    last = nc.tensor.matmul(bank, q_lo[p][:, qs], k_hi[p][:, ks], start=False, stop=True)
                last.then_inc(scores_done, 1)

            def transpose_probs(c, t, g):
                if g == 0:
                    pe.wait_ge(exp_done, c.upto(QT, t + 1))
                if not (c.known and c.n == 0 and t == 0 and g < 2):
                    pe.wait_ge(p_evac, c.upto(QT * NG, t * NG + g - 1))
                bank = t_ps[g % 2]
                for j, tile in enumerate(group_tiles(g)):
                    r = rows(tile)
                    last = nc.tensor.transpose(bank[0:r, j * P:(j + 1) * P], probs[t][:, tile * P:tile * P + r],
                                               ident[:, :])
                last.then_inc(p_transposed, 1)

            def pv(c, t, g):
                if g == 0 and not (c.known and c.n == 0 and t == 0):
                    pe.wait_ge(u_done, c.upto(QT, t))
                pe.wait_ge(p_evac, c.upto(QT * NG, t * NG + g + 1))
                for j, tile in enumerate(group_tiles(g)):
                    r = rows(tile)
                    last = nc.tensor.matmul(u_ps[:, 0:D], pt[g][0:r, j * P:(j + 1) * P], norm[c.parity][0:r, tile, :],
                                            start=(tile == 0), stop=(tile == KT - 1))
                last.then_inc(pv_done, 1)

            def transpose_keys(c, g):
                pe.wait_ge(norm_done, c.upto(NG, g + 1))
                if g == 0 and not (c.known and c.n == 0):
                    pe.wait_ge(max_done, c.shift(-1).upto(QT, QT))
                if g == NG - 1:
                    pe.wait_ge(q_evac, c.upto(2, 2))
                for j, tile in enumerate(group_tiles(g)):
                    r = rows_repeated(tile)
                    last = nc.tensor.transpose(s_ps[:, g * BANK + j * P:g * BANK + j * P + r], norm[c.parity][0:r, tile, :],
                                               ident[0:r, 0:r])
                last.then_inc(k_transposed, 1)

            def transpose_z(c):
                pe.wait_ge(z_done, c.upto(1, 1))
                if not (c.known and c.n == 0):
                    pe.wait_ge(max_done, c.shift(-1).upto(QT, QT))
                for t in range(QT):
                    last = nc.tensor.transpose(z_ps[:, t * P:(t + 1) * P], z[:, t, :], ident[:, :])
                last.then_inc(z_transposed, 1)

            def transpose_y(c):
                pe.wait_ge(y_done, c.upto(1, 1))
                if not (c.known and c.n == 0):
                    pe.wait_ge(gated_done, c.upto(1, 0))
                for t in range(QT):
                    last = nc.tensor.transpose(m_ps[:, t * P:(t + 1) * P], y[:, t, :], ident[:, :])
                last.then_inc(y_transposed, 1)

            def receptance_and_key(c):
                pe.wait_ge(mixed, c.upto(1, 1))
                for t in range(QT):
                    nc.tensor.matmul(m_ps[:, t * P:(t + 1) * P], mixed_r[:, t * P:(t + 1) * P], w_t[:, 0, :],
                                     start=True, stop=True)
                nc.tensor.matmul(m_ps[:, SQ:2 * SQ], w_t[:, 1, :], mixed_k[:, :], start=True,
                                 stop=True).then_inc(rk_done, 1)

            def value(c):
                pe.wait_ge(gate_done, c.upto(1, 1))
                pe.wait_ge(k_squared, c.upto(1, 1))
                for t in range(QT):
                    last = nc.tensor.matmul(m_ps[:, t * P:(t + 1) * P], k_sq[:, t * P:(t + 1) * P], w_t[:, 2, :],
                                            start=True, stop=True)
                last.then_inc(kv_done, 1)

            def iteration(b):
                nxt, prev, old = b.shift(1), b.shift(-1), b.shift(-2)
                if b.exists():
                    scores(b, 0)
                if prev.exists():
                    transpose_probs(prev, 1, 0)
                    transpose_probs(prev, 1, 1)
                if old.exists():
                    transpose_y(old)
                if prev.exists():
                    pv(prev, 1, 0)
                    transpose_probs(prev, 1, 2)
                    transpose_probs(prev, 1, 3)
                    pv(prev, 1, 1)
                    pv(prev, 1, 2)
                    pv(prev, 1, 3)
                if old.exists():
                    receptance_and_key(old)
                if b.exists():
                    scores(b, 1)
                    transpose_probs(b, 0, 0)
                    transpose_probs(b, 0, 1)
                if old.exists():
                    value(old)
                if b.exists():
                    pv(b, 0, 0)
                    transpose_probs(b, 0, 2)
                    transpose_probs(b, 0, 3)
                if nxt.exists():
                    transpose_z(nxt)
                    transpose_keys(nxt, 0)
                if b.exists():
                    pv(b, 0, 1)
                if nxt.exists():
                    transpose_keys(nxt, 1)
                if b.exists():
                    pv(b, 0, 2)
                if nxt.exists():
                    transpose_keys(nxt, 2)
                    transpose_keys(nxt, 3)
                if b.exists():
                    pv(b, 0, 3)

            pe.wait_ge(w_copied, 1)
            run_pipeline(pe, iteration)

        @block.scalar
        def _(act):
            def column(i):
                return cols[:, i:i + 1]

            act.dma_start(column(INV), inv_scale.broadcast_to([P, 1])).then_inc(consts_in, 16)
            for i, v in ((W1, w1), (B1, b1), (W2, w2), (B2, b2)):
                act.dma_start(column(i), v.rearrange("(d o) -> d o", o=1)).then_inc(consts_in, 16)
            for i, w in enumerate((W_r, W_k, W_v)):
                act.dma_start(w_raw[:, i, :], w).then_inc(weights_in, 16)
            for i, v in ((MUR, mu_r), (MUK, mu_k)):
                act.dma_start(column(i), v.rearrange("(d o) -> d o", o=1)).then_inc(late_consts_in, 16)
            act.dma_start(column(GX), g_xattn.rearrange("(a o) -> a o", o=1).broadcast_to([P, 1])).then_inc(late_consts_in, 16)
            act.dma_start(column(GF), g_ffn.rearrange("(a o) -> a o", o=1).broadcast_to([P, 1])).then_inc(late_consts_in, 16)
            for t, v in ((w3_bc, w3), (b3_bc, b3), (w4_raw, w4), (b4_raw, b4)):
                act.dma_start(t[:, :], v.rearrange("(o d) -> o d", o=1).broadcast_to([P, D])).then_inc(late_consts_in, 16)
            act.wait_ge(consts_in, 16 * N_CONSTS)
            for p in range(2):
                nc.scalar.activation(k_hi[p][:, SC - 1:SC], column(B2), ACT.Copy).then_inc(b2_high, 1)
            act.wait_ge(late_consts_in, 16 * N_LATE)
            nc.scalar.activation(cols[:, TGX:TGX + 2], cols[:, GX:GX + 2], ACT.Tanh).then_inc(gates_set, 1)
            act.wait_ge(w_transposed, 1)
            nc.scalar.activation(w_t[:, :, :].rearrange("p a d -> p (a d)"), m_ps[:, 0:3 * D],
                                 ACT.Copy).then_inc(w_copied, 1)
            act.wait_ge(dve_consts, 3)

            def copy_probs(c, t, g):
                act.wait_ge(p_transposed, c.upto(QT * NG, t * NG + g + 1))
                if not (c.known and c.n == 0 and t == 0):
                    act.wait_ge(pv_done, c.upto(QT * NG, (t - 1) * NG + g + 1))
                tiles = group_tiles(g)
                r, n = rows(tiles[-1]), len(tiles) * P
                bank = t_ps[g % 2]
                nc.scalar.activation(pt[g][0:r, 0:n], bank[0:r, 0:n], ACT.Copy).then_inc(p_evac, 1)

            def exponentials(c, t):
                act.wait_ge(max_done, c.upto(QT, t + 1))
                if not (c.known and c.n == 0):
                    act.wait_ge(p_transposed, c.shift(-1).upto(QT * NG, (t + 1) * NG))
                    act.wait_ge(sums_inv, c.shift(-1).upto(QT, t + 1))
                nc.scalar.activation(probs[t][:, :], neg_s[t][:, 0:SK], ACT.Exp, bias=neg_max[:, t:t + 1], scale=-1.0,
                                     accum_out=sums[:, t:t + 1]).then_inc(exp_done, 1)

            def store(c):
                act.wait_ge(result_done, c.upto(1, 1))
                act.dma_start(out_tiles[c.n], result[c.parity][:, :, :]).then_inc(stored[c.parity], 16)

            def high_keys(c, g):
                act.wait_ge(k_transposed, c.upto(NG, g + 1))
                lo, hi = group_columns(g)
                nc.scalar.activation(k_hi[c.parity][:, lo:hi], s_ps[:, g * BANK:g * BANK + hi - lo], ACT.Copy,
                                     scale=column(W2)).then_inc(k_high, 1)

            def queries(c):
                act.wait_ge(z_transposed, c.upto(1, 1))
                if not (c.known and c.n == 0):
                    act.wait_ge(q_done, c.upto(1, 0))
                nc.scalar.activation(q_full[:, :], z_ps, ACT.Identity, bias=column(B1S),
                                     scale=column(W1S)).then_inc(q_evac, 1)
                nc.scalar.activation(q_hi[c.parity][:, :], z_ps, ACT.Identity, bias=column(B1S),
                                     scale=column(W1S)).then_inc(q_evac, 1)

            def attention_out(c, t):
                act.wait_ge(pv_done, c.upto(QT * NG, (t + 1) * NG))
                act.wait_ge(sums_inv, c.upto(QT, t + 1))
                if t == 0 and not (c.known and c.n == 0):
                    act.wait_ge(o_steps, c.upto(4, -3))
                nc.scalar.activation(u[:, t, :], u_ps[:, 0:D], ACT.Copy,
                                     scale=inv_sums[:, t:t + 1]).then_inc(u_done, 1)

            def copy_y(c):
                act.wait_ge(y_transposed, c.upto(1, 1))
                if not (c.known and c.n == 0):
                    act.wait_ge(mixed, c.upto(1, 0))
                nc.scalar.activation(y_t[:, 1:1 + SQ], m_ps[:, 0:SQ], ACT.Copy).then_inc(y_evac, 1)

            def gate_and_relu(c):
                act.wait_ge(rk_done, c.upto(1, 1))
                if not (c.known and c.n == 0):
                    act.wait_ge(gated_done, c.upto(1, 0))
                nc.scalar.activation(k_relu[:, :], m_ps[:, SQ:2 * SQ], ACT.Relu).then_inc(relu_done, 1)
                nc.scalar.activation(gate[:, :, :].rearrange("p t d -> p (t d)"), m_ps[:, 0:SQ], ACT.Tanh,
                                     scale=0.5).then_inc(gate_done, 1)
                act.wait_ge(relu_done, c.upto(1, 1))
                nc.scalar.activation(k_sq[:, :], k_relu[:, :], ACT.Square).then_inc(k_squared, 1)

            def iteration(b):
                nxt, prev, old = b.shift(1), b.shift(-1), b.shift(-2)
                if prev.exists():
                    copy_probs(prev, 1, 0)
                if old.exists():
                    copy_y(old)
                if prev.exists():
                    copy_probs(prev, 1, 1)
                    copy_probs(prev, 1, 2)
                    copy_probs(prev, 1, 3)
                if b.exists():
                    exponentials(b, 0)
                if prev.exists():
                    attention_out(prev, 1)
                if old.exists():
                    gate_and_relu(old)
                if b.exists():
                    copy_probs(b, 0, 0)
                    copy_probs(b, 0, 1)
                    copy_probs(b, 0, 2)
                    copy_probs(b, 0, 3)
                if nxt.exists():
                    queries(nxt)
                    for g in range(NG):
                        high_keys(nxt, g)
                if old.exists():
                    store(old)
                if b.exists():
                    exponentials(b, 1)
                    attention_out(b, 0)

            run_pipeline(act, iteration)

        @block.vector
        def _(dve):
            def column(i):
                return cols[:, i:i + 1]

            def query_and_key_constants():
                dve.wait_ge(consts_in, 16 * N_CONSTS)
                nc.vector.reciprocal(column(RINV), column(INV)).then_inc(dve_consts, 1)
                dve.wait_ge(dve_consts, 1)
                nc.vector.tensor_scalar(column(W1S), column(W1), column(RINV), -1.0, ALU.mult,
                                        ALU.mult).then_inc(dve_consts, 1)
                nc.vector.tensor_scalar(column(B1S), column(B1), column(RINV), -1.0, ALU.mult,
                                        ALU.mult).then_inc(dve_consts, 1)
                dve.wait_ge(b2_high, 2)
                for p in range(2):
                    nc.vector.tensor_tensor(k_lo[p][:, SC - 1:SC], column(B2), k_hi[p][:, SC - 1:SC].bitcast(f32),
                                            ALU.subtract).then_inc(dve_consts, 1)

            def gate_constants():
                dve.wait_ge(gates_set, 1)
                nc.vector.tensor_scalar(column(TGFH), column(TGF), 0.5, None, ALU.mult).then_inc(dve_consts, 1)
                nc.vector.tensor_scalar(w4_bc[:, :], w4_raw[:, :], column(TGX), None, ALU.mult).then_inc(dve_consts, 1)
                nc.vector.tensor_scalar(b4_bc[:, :], b4_raw[:, :], column(TGX), None, ALU.mult).then_inc(dve_consts, 1)
                dve.wait_ge(dve_consts, 8)

            def statistics(c, tiles):
                p = c.parity
                if tiles[0] == 0:
                    dve.wait_ge(ctx_head_in[p], c.loads(16))
                    if not (c.known and c.n < 2):
                        dve.wait_ge(combined, c.shift(-2).upto(6, 6))
                if tiles[0] == HEAD:
                    dve.wait_ge(ctx_tail_in[p], c.loads(48))
                for t in tiles:
                    r = rows_repeated(t)
                    nc.vector.bn_stats(stats[p][0:r, t, :], raw[p][0:r, t, :])
                if tiles[-1] == KT - 1:
                    dve.wait_ge(xq_in[p], c.loads(16))
                    for t in range(QT):
                        last = nc.vector.bn_stats(stats[p][:, KT + t, :], xq[p][:, t, :])
                    last.then_inc(stats_done, 1)

            def normalise_x(c):
                p = c.parity
                dve.wait_ge(combined, c.upto(6, 6))
                if not (c.known and c.n == 0):
                    dve.wait_ge(z_transposed, c.upto(1, 0))
                for t in range(QT):
                    last = nc.vector.tensor_scalar(z[:, t, :], xq[p][:, t, :], neg_mean[p][:, KT + t:KT + t + 1],
                                                   rstd[p][:, KT + t:KT + t + 1], ALU.add, ALU.mult)
                last.then_inc(z_done, 1)

            def low_queries(c):
                dve.wait_ge(q_evac, c.upto(2, 2))
                nc.vector.tensor_tensor(q_lo[c.parity][:, :], q_full[:, :], q_hi[c.parity][:, :].bitcast(f32),
                                        ALU.subtract).then_inc(q_done, 1)

            def low_keys(c, g):
                dve.wait_ge(k_high, c.upto(NG, g + 1))
                lo, hi = group_columns(g)
                nc.vector.scalar_tensor_tensor(k_lo[c.parity][:, lo:hi], s_ps[:, g * BANK:g * BANK + hi - lo], column(W2),
                                               k_hi[c.parity][:, lo:hi].bitcast(f32), ALU.mult,
                                               ALU.subtract).then_inc(k_done, 1)

            def maximum(c, t):
                dve.wait_ge(scores_done, c.upto(QT, t + 1))
                if not (c.known and c.n == 0):
                    dve.wait_ge(exp_done, c.shift(-1).upto(QT, t + 1))
                windows = s_ps[:, :].rearrange("p (w c) -> p w c", w=NW)[:, :, 0:WINDOW]
                q_b2 = s_ps[:, (NW - 1) * BANK + WINDOW:(NW - 1) * BANK + WINDOW + 1]
                joined = neg_s[t][:, :].rearrange("p (w c) -> p w c", w=NW)
                nc.vector.tensor_scalar(joined, windows, q_b2, None, ALU.add, ALU.min,
                                        accum_out=neg_max[:, t:t + 1]).then_inc(max_done, 1)

            def invert_sums(c, t):
                dve.wait_ge(exp_done, c.upto(QT, t + 1))
                if not (c.known and c.n == 0):
                    dve.wait_ge(u_done, c.shift(-1).upto(QT, t + 1))
                nc.vector.reciprocal(inv_sums[:, t:t + 1], sums[:, t:t + 1]).then_inc(sums_inv, 1)

            def times_w3(c):
                dve.wait_ge(u_done, c.upto(QT, QT))
                nc.vector.tensor_tensor(o3[:, :, :], u[:, :, :], w3_bc[:, :].unsqueeze(1).broadcast_to([P, QT, D]),
                                        ALU.mult).then_inc(o_steps, 1)

            def plus_b3(c):
                dve.wait_ge(o_steps, c.upto(4, 1))
                nc.vector.tensor_tensor(o[:, :, :], o3[:, :, :], b3_bc[:, :].unsqueeze(1).broadcast_to([P, QT, D]),
                                        ALU.add).then_inc(o_steps, 1)

            def statistics_o(c):
                dve.wait_ge(o_steps, c.upto(4, 2))
                for t in range(QT):
                    last = nc.vector.bn_stats(st4[:, t, :], o[:, t, :])
                last.then_inc(o_steps, 1)

            def aggregate_o(c):
                dve.wait_ge(o_steps, c.upto(4, 3))
                if not (c.known and c.n == 0):
                    dve.wait_ge(ln_rstd, c.upto(2, -1))
                dve.sem_inc(dve_held, 1)
                for t in range(QT):
                    last = nc.vector.bn_aggr(mv4[:, t, :], st4[:, t, :])
                last.then_inc(o_steps, 1)

            def centre_o(c):
                dve.wait_ge(o_steps, c.upto(4, 4))
                for t in range(QT):
                    last = nc.vector.scalar_tensor_tensor(a4[:, t, :], o[:, t, :], mv4[:, t, 0:1], w4_bc[:, :],
                                                          ALU.subtract, ALU.mult)
                last.then_inc(x1_steps, 1)

            def add_residual(c):
                dve.wait_ge(x1_steps, c.upto(4, 1))
                dve.wait_ge(ln_rstd, c.upto(2, 1))
                dve.wait_ge(xb_done, c.upto(1, 1))
                for t in range(QT):
                    last = nc.vector.scalar_tensor_tensor(x1[c.parity][:, t, :], a4[:, t, :], r4[:, t:t + 1],
                                                          xb[:, t, :], ALU.mult, ALU.add)
                last.then_inc(x1_steps, 1)

            def statistics_x1(c):
                dve.wait_ge(x1_steps, c.upto(4, 2))
                for t in range(QT):
                    last = nc.vector.bn_stats(st5[:, t, :], x1[c.parity][:, t, :])
                last.then_inc(x1_steps, 1)

            def aggregate_x1(c):
                dve.wait_ge(x1_steps, c.upto(4, 3))
                dve.sem_inc(dve_held, 1)
                for t in range(QT):
                    last = nc.vector.bn_aggr(mv5[:, t, :], st5[:, t, :])
                last.then_inc(x1_steps, 1)

            def normalise_x1(c):
                dve.wait_ge(x1_steps, c.upto(4, 4))
                dve.wait_ge(ln_rstd, c.upto(2, 2))
                if not (c.known and c.n == 0):
                    dve.wait_ge(y_transposed, c.upto(1, 0))
                for t in range(QT):
                    last = nc.vector.tensor_scalar(y[:, t, :], x1[c.parity][:, t, :], mv5[:, t, 0:1], r5[:, t:t + 1],
                                                   ALU.subtract, ALU.mult)
                last.then_inc(y_done, 1)

            def mix(c):
                dve.wait_ge(y_evac, c.upto(1, 1))
                nc.vector.tensor_tensor(dy[:, :], y_t[:, 1:1 + SQ], y_t[:, 0:SQ], ALU.subtract).then_inc(dy_done, 1)
                dve.wait_ge(dy_done, c.upto(1, 1))
                if not (c.known and c.n == 0):
                    dve.wait_ge(rk_done, c.upto(1, 0))
                nc.vector.scalar_tensor_tensor(mixed_r[:, :], dy[:, :], column(MUR), y_t[:, 0:SQ], ALU.mult, ALU.add)
                nc.vector.scalar_tensor_tensor(mixed_k[:, :], dy[:, :], column(MUK), y_t[:, 0:SQ], ALU.mult,
                                               ALU.add).then_inc(mixed, 1)

            def gated_value(c):
                dve.wait_ge(kv_done, c.upto(1, 1))
                nc.vector.scalar_tensor_tensor(gated[:, :, :].rearrange("p t d -> p (t d)"),
                                               gate[:, :, :].rearrange("p t d -> p (t d)"), 1.0, m_ps[:, 0:SQ],
                                               ALU.add, ALU.mult).then_inc(gated_done, 1)

            def final(c):
                dve.wait_ge(gated_done, c.upto(1, 1))
                if not (c.known and c.n < 2):
                    dve.wait_ge(stored[c.parity], c.shift(-2).loads(16))
                nc.vector.scalar_tensor_tensor(result[c.parity][:, :, :], gated[:, :, :], column(TGFH),
                                               x1[c.parity][:, :, :], ALU.mult, ALU.add).then_inc(result_done, 1)

            def iteration(b):
                nxt, prev, old, new = b.shift(1), b.shift(-1), b.shift(-2), b.shift(2)

                if b.known and b.n == -AHEAD:
                    dve.wait_ge(pool_consts, 4)
                if b.known and b.n == -1:
                    query_and_key_constants()
                if b.known and b.n == 1:
                    gate_constants()

                def do(step, batch, *rest):
                    if batch.exists():
                        step(batch, *rest)

                do(normalise_x1, old)
                do(statistics, new, range(0, 5))
                do(invert_sums, prev, 1)
                do(maximum, b, 0)
                do(mix, old)
                do(statistics, new, range(5, 8))
                do(normalise_x, nxt)
                do(times_w3, prev)
                do(statistics, new, range(8, 9))
                do(plus_b3, prev)
                do(statistics, new, range(9, 10))
                do(statistics_o, prev)
                do(statistics, new, range(10, 11))
                do(aggregate_o, prev)
                do(invert_sums, b, 0)
                do(statistics, new, range(11, KT))
                do(maximum, b, 1)
                do(gated_value, old)
                do(centre_o, prev)
                do(final, old)
                do(add_residual, prev)
                do(low_queries, nxt)
                do(statistics_x1, prev)
                do(low_keys, nxt, 0)
                do(aggregate_x1, prev)
                do(low_keys, nxt, 1)
                do(low_keys, nxt, 2)
                do(low_keys, nxt, 3)

            run_pipeline(dve, iteration)


_INS = ["x", "ctx_1024", "g_xattn", "g_ffn", "L0_xattn_inv_scale_factor", "L0_xattn_ln1_w", "L0_xattn_ln1_b",
        "L0_xattn_ln2_w", "L0_xattn_ln2_b", "L0_xattn_ln3_w", "L0_xattn_ln3_b", "L0_xattn_ln4_w", "L0_xattn_ln4_b",
        "L0_ffn_W_r", "L0_ffn_W_k", "L0_ffn_W_v", "L0_ffn_mu_r", "L0_ffn_mu_k"]


def kernel(**inputs):
    import numpy as _np
    import concourse.bacc as _bacc
    from concourse import mybir as _mybir
    from concourse.bass_utils import run_bass_kernel_spmd as _run

    nc = _bacc.Bacc("TRN2", target_bir_lowering=False, num_devices=1)
    arrays, args = {}, []
    for name in _INS:
        a = _np.ascontiguousarray(inputs[name])
        arrays[f"in_{name}"] = a
        args.append(nc.dram_tensor(f"in_{name}", a.shape, _mybir.dt.from_np(a.dtype), kind="ExternalInput").ap())
    out = nc.dram_tensor("out_x", (B, SQ, D), _mybir.dt.float32, kind="ExternalOutput").ap()
    build(nc, *args, out)
    r = _run(nc, [arrays], core_ids=[0])
    return r.results[0]["out_x"]
```

```python
import concourse.bass as bass
from concourse import mybir
from contextlib import ExitStack

B, SQ, SK, D = 16, 256, 1601, 128
P = 128
QT = SQ // P
KT = -(-SK // P)
KF = SK // P
KR = SK - KF * P
GROUP = 4
NG = -(-KT // GROUP)
HEAD = 2 * GROUP
NW, BANK = 4, 512
WINDOW = -(-SK // NW)
REP = NW * WINDOW - SK
SC = NW * WINDOW + 1
EPS = 1e-5
LAG = 2
AHEAD = 2


class Batch:

    def __init__(self, n, half, parity, known):
        self.n, self.half, self.parity, self.known = n, half, parity, known

    def shift(self, k):
        q = self.parity + k
        return Batch(self.n + k, self.half + q // 2, q % 2, self.known)

    def exists(self):
        return not self.known or 0 <= self.n < B

    def upto(self, per_batch, done):
        return self.n * per_batch + done

    def loads(self, per_batch):
        return (self.half + 1) * per_batch


def run_pipeline(engine, iteration):
    first, last = LAG, B - AHEAD
    for n in range(-AHEAD, first):
        iteration(Batch(n, n // 2, n % 2, True))
    with engine.Fori(first // 2, last // 2) as half:
        for parity in range(2):
            iteration(Batch(half * 2 + parity, half, parity, False))
    for n in range(last, B + LAG):
        iteration(Batch(n, n // 2, n % 2, True))


BOTH, AHEAD_TILE, LAST_TILE = slice(0, QT), slice(0, 1), slice(1, QT)


def build(nc, x, ctx, g_xattn, g_ffn, inv_scale, w1, b1, w2, b2, w3, b3, w4, b4, W_r, W_k, W_v, mu_r, mu_k, out):
    f32, f32r = mybir.dt.float32, mybir.dt.float32r
    ALU, ACT = mybir.AluOpType, mybir.ActivationFunctionType
    x_tiles = x.rearrange("b (t p) d -> b p t d", p=P)
    out_tiles = out.rearrange("b (t p) d -> b p t d", p=P)
    ctx_full = ctx[:, 0:KF * P, :].rearrange("b (p t) d -> b p t d", t=KF)
    ctx_rest = ctx[:, KF * P:SK, :]
    ctx_repeat = ctx[:, 0:REP, :]

    with ExitStack() as stack:
        def sb(name, shape, dt=f32):
            return stack.enter_context(nc.sbuf_tensor(name, shape, dt))

        def two(name, shape, dt=f32):
            return [sb(f"{name}{i}", shape, dt) for i in range(2)]

        def sem(name):
            return stack.enter_context(nc.semaphore(name))

        ident = sb("ident", [P, P])
        cols = sb("cols", [P, 16])
        W1, B1, W2, B2, MUR, MUK, INV, GX, GF = range(9)
        W1S, B1S, RINV, TGX, TGF, TGFH = range(9, 15)
        w_raw = sb("w_raw", [P, 3, D])
        w_t = sb("w_t", [P, 3, D])
        w3_bc, b3_bc = sb("w3_bc", [P, D]), sb("b3_bc", [P, D])
        w4_raw, b4_raw = sb("w4_raw", [P, D]), sb("b4_raw", [P, D])
        w4_bc, b4_bc = sb("w4_bc", [P, D]), sb("b4_bc", [P, D])
        minus_half = sb("minus_half", [P, 1])
        raw = two("raw", [P, KT, D])
        norm = two("norm", [P, KT, D])
        xq = two("xq", [P, QT, D])
        xres = two("xres", [P, QT, D])
        stats = two("stats", [P, KT + QT, 6])
        NS = KT + QT
        neg_mean = two("neg_mean", [P, NS])
        rstd = two("rstd", [P, NS])
        k_hi, k_lo = two("k_hi", [P, SC], f32r), two("k_lo", [P, SC], f32r)
        q_hi, q_lo = two("q_hi", [P, SQ], f32r), two("q_lo", [P, SQ], f32r)
        x1 = two("x1", [P, QT, D])
        result = two("result", [P, QT, D])
        z = sb("z", [P, QT, D])
        q_full = sb("q_full", [P, SQ])
        neg_s = two("neg_s", [P, NW * WINDOW])
        probs = two("probs", [P, SK])
        neg_max = sb("neg_max", [P, QT])
        sums = sb("sums", [P, QT])
        inv_sums = sb("inv_sums", [P, QT])
        pt = [sb(f"pt{g}", [P, GROUP * P]) for g in range(NG)]
        mix_a = sb("mix_a", [P, NS])
        mix_b = sb("mix_b", [P, NS])
        mix_c = sb("mix_c", [P, NS])
        mix_d = sb("mix_d", [P, NS])
        u = sb("u", [P, QT, D])
        o = sb("o", [P, QT, D])
        o3 = sb("o3", [P, QT, D])
        a4 = sb("a4", [P, QT, D])
        xb = sb("xb", [P, QT, D])
        st4, mv4, ve4, r4 = sb("st4", [P, QT, 6]), sb("mv4", [P, QT, 2]), sb("ve4", [P, QT]), sb("r4", [P, QT])
        st5, mv5, ve5, r5 = sb("st5", [P, QT, 6]), sb("mv5", [P, QT, 2]), sb("ve5", [P, QT]), sb("r5", [P, QT])
        y = sb("y", [P, QT, D])
        y_t = sb("y_t", [P, 1 + SQ])
        dy = sb("dy", [P, SQ])
        mixed_r, mixed_k = sb("mixed_r", [P, SQ]), sb("mixed_k", [P, SQ])
        gate = sb("gate", [P, QT, D])
        k_relu, k_sq = sb("k_relu", [P, SQ]), sb("k_sq", [P, SQ])
        gated = sb("gated", [P, QT, D])

        s_ps = stack.enter_context(nc.psum_tensor("s_ps", [P, NW * BANK], f32))
        t_ps = [stack.enter_context(nc.psum_tensor(f"t_ps{i}", [P, GROUP * P], f32)) for i in range(2)]
        z_ps = s_ps[:, (NW - 1) * BANK + P:(NW - 1) * BANK + P + SQ]
        u_ps = stack.enter_context(nc.psum_tensor("u_ps", [P, 512], f32))
        m_ps = stack.enter_context(nc.psum_tensor("m_ps", [P, 512], f32))

        consts_in = sem("consts_in")
        weights_in = sem("weights_in")
        late_consts_in = sem("late_consts_in")
        ident_set = sem("ident_set")
        pool_consts = sem("pool_consts")
        gates_set = sem("gates_set")
        dve_consts = sem("dve_consts")
        w_transposed = sem("w_transposed")
        w_copied = sem("w_copied")
        b2_high = sem("b2_high")
        first_group_in = sem("first_group_in")
        ctx_head_in = [sem(f"ctx_head_in{i}") for i in range(2)]
        ctx_tail_in = [sem(f"ctx_tail_in{i}") for i in range(2)]
        xq_in = [sem(f"xq_in{i}") for i in range(2)]
        xres_in = [sem(f"xres_in{i}") for i in range(2)]
        stored = [sem(f"stored{i}") for i in range(2)]
        stats_done = sem("stats_done")
        combined = sem("combined")
        first_rstd = sem("first_rstd")
        norm_done = sem("norm_done")
        z_done = sem("z_done")
        z_transposed = sem("z_transposed")
        q_evac = sem("q_evac")
        q_high = sem("q_high")
        q_done = sem("q_done")
        k_transposed = sem("k_transposed")
        k_high = sem("k_high")
        k_done = sem("k_done")
        scores_done = sem("scores_done")
        max_done = sem("max_done")
        exp_done = sem("exp_done")
        sums_inv = sem("sums_inv")
        p_transposed = sem("p_transposed")
        p_evac = sem("p_evac")
        pv_done = sem("pv_done")
        u_done = sem("u_done")
        o_steps = sem("o_steps")
        xb_done = sem("xb_done")
        eps_added = sem("eps_added")
        ln_rstd = sem("ln_rstd")
        x1_steps = sem("x1_steps")
        ahead_steps = sem("ahead_steps")
        ahead_roots = sem("ahead_roots")
        y_done = sem("y_done")
        y_transposed = sem("y_transposed")
        y_evac = sem("y_evac")
        dy_done = sem("dy_done")
        mixed = sem("mixed")
        rk_done = sem("rk_done")
        gate_done = sem("gate_done")
        relu_done = sem("relu_done")
        k_squared = sem("k_squared")
        kv_done = sem("kv_done")
        gated_done = sem("gated_done")
        result_done = sem("result_done")
        pool_held = sem("pool_held")
        dve_held = sem("dve_held")

        N_CONSTS, N_WEIGHTS, N_LATE = 5, 3, 8
        block = stack.enter_context(nc.Block())

        def group_tiles(g):
            return range(g * GROUP, min((g + 1) * GROUP, KT))

        def rows(tile):
            return KR if tile == KT - 1 else P

        def rows_repeated(tile):
            return KR + REP if tile == KT - 1 else P

        def group_columns(g):
            lo = g * GROUP * P
            return lo, min(lo + GROUP * P, SC - 1)

        def o_step(c, tiles, k):
            return (ahead_steps, k) if tiles == AHEAD_TILE else (o_steps, c.upto(4, k))

        def x1_step(c, tiles, k):
            return (ahead_steps, 4 + k) if tiles == AHEAD_TILE else (x1_steps, c.upto(4, k))

        def rstd_step(c, tiles, which):
            return (ahead_roots, 2 * which + 2) if tiles == AHEAD_TILE else (ln_rstd, c.upto(2, which + 1))

        @block.sync
        def _(sp):
            def load_head(c):
                p = c.parity
                if not (c.known and c.n < 2):
                    sp.wait_ge(norm_done, c.shift(-2).upto(NG, 2))
                first = 0
                if c.known and c.n == 0:
                    first = GROUP
                    sp.dma_start(raw[p][:, 0:GROUP, :], ctx_full[c.n, :, 0:GROUP, :]).then_inc(first_group_in, 16)
                sp.dma_start(raw[p][:, first:HEAD, :], ctx_full[c.n, :, first:HEAD, :]).then_inc(ctx_head_in[p], 16)

            def load_tail(c):
                p = c.parity
                if not (c.known and c.n < 2):
                    sp.wait_ge(norm_done, c.shift(-2).upto(NG, NG))
                sp.dma_start(raw[p][:, HEAD:KF, :], ctx_full[c.n, :, HEAD:KF, :]).then_inc(ctx_tail_in[p], 16)
                sp.dma_start(raw[p][0:KR, KF, :], ctx_rest[c.n]).then_inc(ctx_tail_in[p], 16)
                sp.dma_start(raw[p][KR:KR + REP, KF, :], ctx_repeat[c.n]).then_inc(ctx_tail_in[p], 16)

            def load_xq(c):
                if not (c.known and c.n < 2):
                    sp.wait_ge(z_done, c.shift(-2).upto(1, 1))
                sp.dma_start(xq[c.parity][:, :, :], x_tiles[c.n]).then_inc(xq_in[c.parity], 16)

            def load_xres(c):
                if not (c.known and c.n < 2):
                    sp.wait_ge(xb_done, c.shift(-2).upto(1, 1))
                sp.dma_start(xres[c.parity][:, :, :], x_tiles[c.n]).then_inc(xres_in[c.parity], 16)

            def load_late_constants():
                for i, w in enumerate((W_r, W_k, W_v)):
                    sp.dma_start(w_raw[:, i, :], w).then_inc(weights_in, 16)
                for i, v in ((MUR, mu_r), (MUK, mu_k)):
                    sp.dma_start(cols[:, i:i + 1], v.rearrange("(d o) -> d o", o=1)).then_inc(late_consts_in, 16)
                for i, g in ((GX, g_xattn), (GF, g_ffn)):
                    sp.dma_start(cols[:, i:i + 1], g.rearrange("(a o) -> a o", o=1).broadcast_to([P, 1])).then_inc(
                        late_consts_in, 16)
                for t, v in ((w3_bc, w3), (b3_bc, b3), (w4_raw, w4), (b4_raw, b4)):
                    sp.dma_start(t[:, :], v.rearrange("(o d) -> o d", o=1).broadcast_to([P, D])).then_inc(late_consts_in, 16)

            def iteration(b):
                if b.known and b.n == 0:
                    load_late_constants()
                if b.shift(2).exists():
                    load_head(b.shift(2))
                    load_tail(b.shift(2))
                    load_xq(b.shift(2))
                if b.exists():
                    load_xres(b)

            run_pipeline(sp, iteration)
            for p in range(2):
                sp.wait_ge(stored[p], 16 * (B // 2))

        @block.gpsimd
        def _(pool):
            nc.gpsimd.memset(ident[:, :], 0.0).then_inc(ident_set, 1)
            nc.gpsimd.memset(minus_half[:, :], -0.5).then_inc(pool_consts, 1)
            for p in range(2):
                nc.gpsimd.memset(stats[p][:, :, :], 1.0).then_inc(pool_consts, 1)
            nc.gpsimd.memset(y_t[:, 0:1], 0.0).then_inc(pool_consts, 1)
            pool.wait_ge(ident_set, 1)
            nc.gpsimd.affine_select(out=ident[:, :], in_=ident[:, :], compare_op=ALU.not_equal, fill=1.0, base=0,
                                    pattern=[[-1, P]], channel_multiplier=1).then_inc(ident_set, 1)
            pool.wait_ge(pool_consts, 4)

            def stand_alone():
                pool.sem_inc(pool_held, 1)

            def combine(c):
                st, xs = stats[c.parity], slice(KT, NS)
                mean_e, m2_e, mean_o, m2_o = st[:, :, 1], st[:, :, 2], st[:, :, 4], st[:, :, 5]
                steps = 6
                pool.wait_ge(stats_done, c.upto(1, 1))
                nc.gpsimd.tensor_tensor(mix_a[:, :], mean_e, mean_o, ALU.add)
                nc.gpsimd.tensor_tensor(mix_b[:, :], mean_e, mean_o, ALU.subtract)
                nc.gpsimd.tensor_tensor(mix_c[:, :], m2_e, m2_o, ALU.add).then_inc(combined, 1)
                pool.wait_ge(combined, c.upto(steps, 1))
                nc.gpsimd.tensor_tensor(mix_d[:, :], mix_b[:, :], mix_b[:, :], ALU.mult)
                nc.gpsimd.tensor_scalar(neg_mean[c.parity][:, :], mix_a[:, :], -0.5, 0.0, ALU.mult,
                                        ALU.add).then_inc(combined, 1)
                pool.wait_ge(combined, c.upto(steps, 2))
                stand_alone()
                nc.gpsimd.tensor_scalar(mix_b[:, :], mix_d[:, :], 0.25, 0.0, ALU.mult, ALU.add)
                nc.gpsimd.tensor_scalar(mix_a[:, :], mix_c[:, :], 1.0 / D, 0.0, ALU.mult, ALU.add).then_inc(combined, 1)
                pool.wait_ge(combined, c.upto(steps, 3))
                nc.gpsimd.tensor_tensor(mix_d[:, :], mix_a[:, :], mix_b[:, :], ALU.add).then_inc(combined, 1)
                pool.wait_ge(combined, c.upto(steps, 4))
                stand_alone()
                nc.gpsimd.tensor_scalar(mix_c[:, 0:KT], mix_d[:, 0:KT], 1.0, EPS, ALU.mult, ALU.add)
                nc.gpsimd.tensor_scalar(mix_c[:, xs], mix_d[:, xs], 1.0 + EPS, EPS * EPS, ALU.mult,
                                        ALU.add).then_inc(combined, 1)
                pool.wait_ge(combined, c.upto(steps, 5))
                nc.gpsimd.tensor_tensor(rstd[c.parity][:, :], mix_c[:, :], minus_half[:, :].broadcast_to([P, NS]),
                                        ALU.pow).then_inc(combined, 1)

            def first_roots():
                pool.wait_ge(combined, 5)
                stand_alone()
                for lo, hi in [(KT, NS)] + [(g * GROUP, min((g + 1) * GROUP, KT)) for g in range(NG)]:
                    nc.gpsimd.tensor_tensor(rstd[0][:, lo:hi], mix_c[:, lo:hi], minus_half[:, :].broadcast_to([P, hi - lo]),
                                            ALU.pow).then_inc(first_rstd, 1)
                pool.wait_ge(first_rstd, 1 + NG)
                pool.sem_inc(combined, 1)

            def normalise(c, g):
                p = c.parity
                if g == 0:
                    pool.wait_ge(combined, c.upto(6, 6))
                    if c.known and c.n < 2:
                        stand_alone()
                if not (c.known and c.n < 2):
                    pool.wait_ge(pv_done, c.shift(-2).upto(QT * NG, NG + g + 1))
                    stand_alone()
                for t in group_tiles(g):
                    r = rows_repeated(t)
                    last = nc.gpsimd.tensor_scalar(norm[p][0:r, t, :], raw[p][0:r, t, :], neg_mean[p][0:r, t:t + 1],
                                                   rstd[p][0:r, t:t + 1], ALU.add, ALU.mult)
                last.then_inc(norm_done, 1)

            def residual_with_bias(c):
                if c.known and c.n == 0:
                    pool.wait_ge(dve_consts, 8)
                pool.wait_ge(xres_in[c.parity], c.loads(16))
                if not (c.known and c.n < 1):
                    pool.wait_ge(x1_steps, c.shift(-1).upto(4, 2))
                nc.gpsimd.tensor_tensor(xb[:, :, :], xres[c.parity][:, :, :],
                                        b4_bc[:, :].unsqueeze(1).broadcast_to([P, QT, D]), ALU.add).then_inc(xb_done, 1)

            def root(c, which, tiles=BOTH):
                mv, ve, r = ((mv4, ve4, r4), (mv5, ve5, r5))[which]
                pool.wait_ge(*(x1_step if which else o_step)(c, tiles, 4))
                stand_alone()
                done, value = rstd_step(c, tiles, which)
                added, added_value = (done, value - 1) if tiles == AHEAD_TILE else (eps_added, value)
                nc.gpsimd.tensor_scalar(ve[:, tiles], mv[:, tiles, 1], 1.0, EPS, ALU.mult, ALU.add).then_inc(added, 1)
                pool.wait_ge(added, added_value)
                nc.gpsimd.tensor_tensor(r[:, tiles], ve[:, tiles],
                                        minus_half[:, :].broadcast_to([P, tiles.stop - tiles.start]),
                                        ALU.pow).then_inc(done, 1)

            def iteration(b):
                nxt, prev = b.shift(1), b.shift(-1)
                if b.known and b.n == -1:
                    first_roots()
                    pool.wait_ge(norm_done, 2)
                    stand_alone()
                    normalise(nxt, 2)
                    normalise(nxt, 3)
                    return
                if b.known and b.n == B:
                    residual_with_bias(prev)
                    root(prev, 0, AHEAD_TILE)
                    root(prev, 1, AHEAD_TILE)
                    root(prev, 0, LAST_TILE)
                    root(prev, 1, LAST_TILE)
                    return
                if nxt.exists():
                    combine(nxt)
                    normalise(nxt, 0)
                    normalise(nxt, 1)
                if prev.exists():
                    root(prev, 0)
                    residual_with_bias(prev)
                if nxt.exists():
                    normalise(nxt, 2)
                    normalise(nxt, 3)
                if prev.exists():
                    root(prev, 1)

            run_pipeline(pool, iteration)

        @block.tensor
        def _(pe):
            pe.wait_ge(ident_set, 2)

            def transpose_weights():
                pe.wait_ge(weights_in, 16 * N_WEIGHTS)
                for i in range(3):
                    last = nc.tensor.transpose(m_ps[:, i * D:(i + 1) * D], w_raw[:, i, :], ident[:, :])
                last.then_inc(w_transposed, 1)

            def keep_clock_up(products):
                for _ in range(products):
                    nc.tensor.matmul(t_ps[1][:, 0:P], ident[:, :], ident[:, :], start=True, stop=True)

            def scores(c, t):
                p = c.parity
                if t == 0:
                    pe.wait_ge(q_done, c.upto(1, 1))
                if not (c.known and c.n == 0 and t == 0):
                    pe.wait_ge(max_done, c.upto(QT, t))
                qs = slice(t * P, (t + 1) * P)
                for i in range(NW):
                    lo = i * WINDOW
                    ks = slice(lo, lo + WINDOW + 1)
                    if t == 0:
                        pe.wait_ge(k_done, c.upto(NG, min(-(-(lo + WINDOW + 1) // (GROUP * P)), NG)))
                    bank = s_ps[:, i * BANK:i * BANK + WINDOW + 1]
                    nc.tensor.matmul(bank, q_hi[p][:, qs], k_hi[p][:, ks], start=True, stop=False)
                    nc.tensor.matmul(bank, q_hi[p][:, qs], k_lo[p][:, ks], start=False, stop=False)
                    last = nc.tensor.matmul(bank, q_lo[p][:, qs], k_hi[p][:, ks], start=False, stop=True)
                last.then_inc(scores_done, 1)

            def transpose_probs(c, t, g):
                if g == 0:
                    pe.wait_ge(exp_done, c.upto(QT, t + 1))
                if not (c.known and c.n == 0 and t == 0 and g < 2):
                    pe.wait_ge(p_evac, c.upto(QT * NG, t * NG + g - 1))
                bank = t_ps[g % 2]
                for j, tile in enumerate(group_tiles(g)):
                    r = rows(tile)
                    last = nc.tensor.transpose(bank[0:r, j * P:(j + 1) * P], probs[t][:, tile * P:tile * P + r],
                                               ident[:, :])
                last.then_inc(p_transposed, 1)

            def pv(c, t, g):
                if g == 0 and not (c.known and c.n == 0 and t == 0):
                    pe.wait_ge(u_done, c.upto(QT, t))
                pe.wait_ge(p_evac, c.upto(QT * NG, t * NG + g + 1))
                for j, tile in enumerate(group_tiles(g)):
                    r = rows(tile)
                    last = nc.tensor.matmul(u_ps[:, 0:D], pt[g][0:r, j * P:(j + 1) * P], norm[c.parity][0:r, tile, :],
                                            start=(tile == 0), stop=(tile == KT - 1))
                last.then_inc(pv_done, 1)

            def transpose_keys(c, g):
                pe.wait_ge(norm_done, c.upto(NG, g + 1))
                if g == 0 and not (c.known and c.n == 0):
                    pe.wait_ge(max_done, c.shift(-1).upto(QT, QT))
                if g == NG - 1:
                    pe.wait_ge(q_evac, c.upto(1, 1))
                for j, tile in enumerate(group_tiles(g)):
                    r = rows_repeated(tile)
                    last = nc.tensor.transpose(s_ps[:, g * BANK + j * P:g * BANK + j * P + r], norm[c.parity][0:r, tile, :],
                                               ident[0:r, 0:r])
                last.then_inc(k_transposed, 1)

            def transpose_z(c):
                pe.wait_ge(z_done, c.upto(1, 1))
                if not (c.known and c.n == 0):
                    pe.wait_ge(max_done, c.shift(-1).upto(QT, QT))
                for t in range(QT):
                    last = nc.tensor.transpose(z_ps[:, t * P:(t + 1) * P], z[:, t, :], ident[:, :])
                last.then_inc(z_transposed, 1)

            def transpose_y(c):
                pe.wait_ge(y_done, c.upto(1, 1))
                if not (c.known and c.n == 0):
                    pe.wait_ge(gated_done, c.upto(1, 0))
                for t in range(QT):
                    last = nc.tensor.transpose(m_ps[:, t * P:(t + 1) * P], y[:, t, :], ident[:, :])
                last.then_inc(y_transposed, 1)

            def receptance_and_key(c):
                pe.wait_ge(mixed, c.upto(2, 1))
                nc.tensor.matmul(m_ps[:, SQ:2 * SQ], w_t[:, 1, :], mixed_k[:, :], start=True, stop=True)
                pe.wait_ge(mixed, c.upto(2, 2))
                for t in range(QT):
                    last = nc.tensor.matmul(m_ps[:, t * P:(t + 1) * P], mixed_r[:, t * P:(t + 1) * P], w_t[:, 0, :],
                                            start=True, stop=True)
                last.then_inc(rk_done, 1)

            def value(c):
                pe.wait_ge(gate_done, c.upto(1, 1))
                pe.wait_ge(k_squared, c.upto(1, 1))
                for t in range(QT):
                    last = nc.tensor.matmul(m_ps[:, t * P:(t + 1) * P], k_sq[:, t * P:(t + 1) * P], w_t[:, 2, :],
                                            start=True, stop=True)
                last.then_inc(kv_done, 1)

            def iteration(b):
                nxt, prev, old = b.shift(1), b.shift(-1), b.shift(-2)
                drains, last = b.known and b.n >= B, b.known and b.n == B + 1

                def do(step, batch, *rest):
                    if batch.exists():
                        step(batch, *rest)

                do(scores, b, 0)
                if not drains:
                    do(transpose_y, old)
                do(transpose_probs, prev, 1, 2)
                do(pv, prev, 1, 0)
                if drains:
                    do(transpose_y, old)
                if last:
                    keep_clock_up(7)
                do(transpose_probs, prev, 1, 3)
                do(pv, prev, 1, 1)
                do(pv, prev, 1, 2)
                do(pv, prev, 1, 3)
                do(receptance_and_key, old)
                if drains:
                    keep_clock_up(5)
                if b.known and b.n == 1:
                    transpose_weights()
                if b.known and b.n == 0:
                    keep_clock_up(6)
                    do(scores, b, 1)
                    do(transpose_probs, b, 0, 0)
                else:
                    do(transpose_probs, b, 0, 0)
                    do(scores, b, 1)
                do(transpose_probs, b, 0, 1)
                do(value, old)
                if drains and not last:
                    keep_clock_up(10)
                do(transpose_probs, b, 0, 2)
                do(pv, b, 0, 0)
                do(transpose_probs, b, 0, 3)
                first = b.known and b.n == -1
                if first:
                    pe.wait_ge(stats_done, 1)
                    keep_clock_up(7)
                do(transpose_z, nxt)
                if first:
                    keep_clock_up(2)
                do(transpose_keys, nxt, 0)
                do(pv, b, 0, 1)
                do(transpose_keys, nxt, 1)
                do(pv, b, 0, 2)
                if first:
                    keep_clock_up(4)
                do(transpose_keys, nxt, 2)
                do(transpose_keys, nxt, 3)
                do(pv, b, 0, 3)
                do(transpose_probs, b, 1, 0)
                do(transpose_probs, b, 1, 1)
                if b.known and b.n == 1:
                    pe.wait_ge(w_copied, 1)

            run_pipeline(pe, iteration)

        @block.scalar
        def _(act):
            def column(i):
                return cols[:, i:i + 1]

            act.dma_start(column(B2), b2.rearrange("(d o) -> d o", o=1)).then_inc(consts_in, 16)
            act.dma_start(column(INV), inv_scale.broadcast_to([P, 1])).then_inc(consts_in, 16)
            for i, v in ((W1, w1), (B1, b1), (W2, w2)):
                act.dma_start(column(i), v.rearrange("(d o) -> d o", o=1)).then_inc(consts_in, 16)
            act.wait_ge(consts_in, 16 * N_CONSTS)
            for p in range(2):
                nc.scalar.activation(k_hi[p][:, SC - 1:SC], column(B2), ACT.Copy).then_inc(b2_high, 1)
            act.wait_ge(dve_consts, 3)

            def gates():
                act.wait_ge(late_consts_in, 16 * N_LATE)
                nc.scalar.activation(cols[:, TGX:TGX + 2], cols[:, GX:GX + 2], ACT.Tanh).then_inc(gates_set, 1)

            def copy_weights():
                act.wait_ge(w_transposed, 1)
                nc.scalar.activation(w_t[:, :, :].rearrange("p a d -> p (a d)"), m_ps[:, 0:3 * D],
                                     ACT.Copy).then_inc(w_copied, 1)

            def copy_probs(c, t, g):
                act.wait_ge(p_transposed, c.upto(QT * NG, t * NG + g + 1))
                if not (c.known and c.n == 0 and t == 0):
                    act.wait_ge(pv_done, c.upto(QT * NG, (t - 1) * NG + g + 1))
                tiles = group_tiles(g)
                r, n = rows(tiles[-1]), len(tiles) * P
                bank = t_ps[g % 2]
                nc.scalar.activation(pt[g][0:r, 0:n], bank[0:r, 0:n], ACT.Copy).then_inc(p_evac, 1)

            def exponentials(c, t):
                act.wait_ge(max_done, c.upto(QT, t + 1))
                if not (c.known and c.n == 0):
                    act.wait_ge(p_transposed, c.shift(-1).upto(QT * NG, (t + 1) * NG))
                    act.wait_ge(sums_inv, c.shift(-1).upto(QT, t + 1))
                nc.scalar.activation(probs[t][:, :], neg_s[t][:, 0:SK], ACT.Exp, bias=neg_max[:, t:t + 1], scale=-1.0,
                                     accum_out=sums[:, t:t + 1]).then_inc(exp_done, 1)

            def store(c):
                act.wait_ge(result_done, c.upto(1, 1))
                act.dma_start(out_tiles[c.n], result[c.parity][:, :, :]).then_inc(stored[c.parity], 16)

            def high_keys(c, g):
                act.wait_ge(k_transposed, c.upto(NG, g + 1))
                lo, hi = group_columns(g)
                nc.scalar.activation(k_hi[c.parity][:, lo:hi], s_ps[:, g * BANK:g * BANK + hi - lo], ACT.Copy,
                                     scale=column(W2)).then_inc(k_high, 1)

            def queries(c):
                act.wait_ge(z_transposed, c.upto(1, 1))
                if not (c.known and c.n == 0):
                    act.wait_ge(q_done, c.upto(1, 0))
                nc.scalar.activation(q_full[:, :], z_ps, ACT.Identity, bias=column(B1S),
                                     scale=column(W1S)).then_inc(q_evac, 1)

            def attention_out(c, t):
                act.wait_ge(pv_done, c.upto(QT * NG, (t + 1) * NG))
                act.wait_ge(sums_inv, c.upto(QT, t + 1))
                if t == 0 and not (c.known and c.n == 0):
                    act.wait_ge(o_steps, c.upto(4, -3))
                nc.scalar.activation(u[:, t, :], u_ps[:, 0:D], ACT.Copy,
                                     scale=inv_sums[:, t:t + 1]).then_inc(u_done, 1)

            def copy_y(c):
                act.wait_ge(y_transposed, c.upto(1, 1))
                if not (c.known and c.n == 0):
                    act.wait_ge(mixed, c.upto(2, 0))
                nc.scalar.activation(y_t[:, 1:1 + SQ], m_ps[:, 0:SQ], ACT.Copy).then_inc(y_evac, 1)

            def gate_and_relu(c):
                act.wait_ge(rk_done, c.upto(1, 1))
                if not (c.known and c.n == 0):
                    act.wait_ge(gated_done, c.upto(1, 0))
                nc.scalar.activation(k_relu[:, :], m_ps[:, SQ:2 * SQ], ACT.Relu).then_inc(relu_done, 1)
                nc.scalar.activation(gate[:, :, :].rearrange("p t d -> p (t d)"), m_ps[:, 0:SQ], ACT.Tanh,
                                     scale=0.5).then_inc(gate_done, 1)
                act.wait_ge(relu_done, c.upto(1, 1))
                nc.scalar.activation(k_sq[:, :], k_relu[:, :], ACT.Square).then_inc(k_squared, 1)

            def iteration(b):
                nxt, prev, old = b.shift(1), b.shift(-1), b.shift(-2)

                def do(step, batch, *rest):
                    if batch.exists():
                        step(batch, *rest)

                if b.known and b.n == 1:
                    gates()
                do(copy_probs, prev, 1, 0)
                do(copy_probs, prev, 1, 1)
                do(copy_y, old)
                do(copy_probs, prev, 1, 2)
                do(copy_probs, prev, 1, 3)
                do(exponentials, b, 0)
                do(attention_out, prev, 1)
                if b.known and b.n == 1:
                    copy_weights()
                do(gate_and_relu, old)
                do(copy_probs, b, 0, 0)
                do(copy_probs, b, 0, 1)
                do(copy_probs, b, 0, 2)
                do(copy_probs, b, 0, 3)
                do(queries, nxt)
                do(high_keys, nxt, 0)
                do(exponentials, b, 1)
                for g in range(1, NG):
                    do(high_keys, nxt, g)
                do(store, old)
                do(attention_out, b, 0)

            run_pipeline(act, iteration)

        @block.vector
        def _(dve):
            def column(i):
                return cols[:, i:i + 1]

            def query_and_key_constants():
                dve.wait_ge(consts_in, 16 * N_CONSTS)
                nc.vector.reciprocal(column(RINV), column(INV)).then_inc(dve_consts, 1)
                dve.wait_ge(dve_consts, 1)
                nc.vector.tensor_scalar(column(W1S), column(W1), column(RINV), -1.0, ALU.mult,
                                        ALU.mult).then_inc(dve_consts, 1)
                nc.vector.tensor_scalar(column(B1S), column(B1), column(RINV), -1.0, ALU.mult,
                                        ALU.mult).then_inc(dve_consts, 1)
                dve.wait_ge(b2_high, 2)
                for p in range(2):
                    nc.vector.tensor_tensor(k_lo[p][:, SC - 1:SC], column(B2), k_hi[p][:, SC - 1:SC].bitcast(f32),
                                            ALU.subtract).then_inc(dve_consts, 1)

            def gate_constants():
                dve.wait_ge(gates_set, 1)
                nc.vector.tensor_scalar(column(TGFH), column(TGF), 0.5, None, ALU.mult).then_inc(dve_consts, 1)
                nc.vector.tensor_scalar(w4_bc[:, :], w4_raw[:, :], column(TGX), None, ALU.mult).then_inc(dve_consts, 1)
                nc.vector.tensor_scalar(b4_bc[:, :], b4_raw[:, :], column(TGX), None, ALU.mult).then_inc(dve_consts, 1)
                dve.wait_ge(dve_consts, 8)

            def statistics(c, tiles):
                p = c.parity
                if tiles[0] == 0:
                    if c.known and c.n == 0:
                        dve.wait_ge(first_group_in, 16)
                    else:
                        dve.wait_ge(ctx_head_in[p], c.loads(16))
                    if not (c.known and c.n < 2):
                        dve.wait_ge(combined, c.shift(-2).upto(6, 6))
                for t in tiles:
                    r = rows_repeated(t)
                    if t == GROUP and c.known and c.n == 0:
                        dve.wait_ge(ctx_head_in[p], c.loads(16))
                    if t == HEAD:
                        dve.wait_ge(ctx_tail_in[p], c.loads(48))
                    nc.vector.bn_stats(stats[p][0:r, t, :], raw[p][0:r, t, :])
                if tiles[-1] == KT - 1:
                    dve.wait_ge(xq_in[p], c.loads(16))
                    for t in range(QT):
                        last = nc.vector.bn_stats(stats[p][:, KT + t, :], xq[p][:, t, :])
                    last.then_inc(stats_done, 1)

            def combine_first():
                st, xs = stats[0], slice(KT, NS)
                mean_e, m2_e, mean_o, m2_o = st[:, :, 1], st[:, :, 2], st[:, :, 4], st[:, :, 5]
                dve.wait_ge(stats_done, 1)
                nc.vector.tensor_tensor(mix_b[:, :], mean_e, mean_o, ALU.subtract)
                nc.vector.tensor_tensor(mix_a[:, :], mean_e, mean_o, ALU.add)
                nc.vector.tensor_tensor(mix_c[:, :], m2_e, m2_o, ALU.add).then_inc(combined, 1)
                dve.wait_ge(combined, 1)
                nc.vector.tensor_tensor(mix_d[:, :], mix_b[:, :], mix_b[:, :], ALU.mult)
                nc.vector.tensor_scalar(neg_mean[0][:, :], mix_a[:, :], -0.5, None, ALU.mult).then_inc(combined, 1)
                dve.wait_ge(combined, 2)
                nc.vector.tensor_scalar(mix_b[:, :], mix_d[:, :], 0.25, None, ALU.mult)
                nc.vector.tensor_scalar(mix_a[:, :], mix_c[:, :], 1.0 / D, None, ALU.mult).then_inc(combined, 1)
                dve.wait_ge(combined, 3)
                nc.vector.tensor_tensor(mix_d[:, :], mix_a[:, :], mix_b[:, :], ALU.add).then_inc(combined, 1)
                dve.wait_ge(combined, 4)
                nc.vector.tensor_scalar(mix_c[:, 0:KT], mix_d[:, 0:KT], 1.0, EPS, ALU.mult, ALU.add)
                nc.vector.tensor_scalar(mix_c[:, xs], mix_d[:, xs], 1.0 + EPS, EPS * EPS, ALU.mult,
                                        ALU.add).then_inc(combined, 1)

            def normalise_first(g):
                dve.wait_ge(first_rstd, 2 + g)
                for t in group_tiles(g):
                    r = rows_repeated(t)
                    last = nc.vector.tensor_scalar(norm[0][0:r, t, :], raw[0][0:r, t, :], neg_mean[0][0:r, t:t + 1],
                                                   rstd[0][0:r, t:t + 1], ALU.add, ALU.mult)
                last.then_inc(norm_done, 1)

            def normalise_x(c):
                p = c.parity
                if c.known and c.n == 0:
                    dve.wait_ge(first_rstd, 1)
                else:
                    dve.wait_ge(combined, c.upto(6, 6))
                if not (c.known and c.n == 0):
                    dve.wait_ge(z_transposed, c.upto(1, 0))
                for t in range(QT):
                    last = nc.vector.tensor_scalar(z[:, t, :], xq[p][:, t, :], neg_mean[p][:, KT + t:KT + t + 1],
                                                   rstd[p][:, KT + t:KT + t + 1], ALU.add, ALU.mult)
                last.then_inc(z_done, 1)

            def high_queries(c):
                dve.wait_ge(q_evac, c.upto(1, 1))
                if not (c.known and c.n < 2):
                    dve.wait_ge(scores_done, c.shift(-2).upto(QT, QT))
                nc.vector.tensor_scalar(q_hi[c.parity][:, :], q_full[:, :], 1.0, None, ALU.mult).then_inc(q_high, 1)

            def low_queries(c):
                dve.wait_ge(q_high, c.upto(1, 1))
                nc.vector.tensor_tensor(q_lo[c.parity][:, :], q_full[:, :], q_hi[c.parity][:, :].bitcast(f32),
                                        ALU.subtract).then_inc(q_done, 1)

            def low_keys(c, g):
                dve.wait_ge(k_high, c.upto(NG, g + 1))
                lo, hi = group_columns(g)
                nc.vector.scalar_tensor_tensor(k_lo[c.parity][:, lo:hi], s_ps[:, g * BANK:g * BANK + hi - lo], column(W2),
                                               k_hi[c.parity][:, lo:hi].bitcast(f32), ALU.mult,
                                               ALU.subtract).then_inc(k_done, 1)

            def maximum(c, t):
                dve.wait_ge(scores_done, c.upto(QT, t + 1))
                if not (c.known and c.n == 0):
                    dve.wait_ge(exp_done, c.shift(-1).upto(QT, t + 1))
                windows = s_ps[:, :].rearrange("p (w c) -> p w c", w=NW)[:, :, 0:WINDOW]
                q_b2 = s_ps[:, (NW - 1) * BANK + WINDOW:(NW - 1) * BANK + WINDOW + 1]
                joined = neg_s[t][:, :].rearrange("p (w c) -> p w c", w=NW)
                nc.vector.tensor_scalar(joined, windows, q_b2, None, ALU.add, ALU.min,
                                        accum_out=neg_max[:, t:t + 1]).then_inc(max_done, 1)

            def invert_sums(c, t):
                dve.wait_ge(exp_done, c.upto(QT, t + 1))
                if not (c.known and c.n == 0):
                    dve.wait_ge(u_done, c.shift(-1).upto(QT, t + 1))
                nc.vector.reciprocal(inv_sums[:, t:t + 1], sums[:, t:t + 1]).then_inc(sums_inv, 1)

            def rows_of(vector, tiles):
                return vector[:, :].unsqueeze(1).broadcast_to([P, tiles.stop - tiles.start, D])

            def times_w3(c, tiles=BOTH):
                dve.wait_ge(u_done, c.upto(QT, tiles.stop))
                nc.vector.tensor_tensor(o3[:, tiles, :], u[:, tiles, :], rows_of(w3_bc, tiles),
                                        ALU.mult).then_inc(o_step(c, tiles, 1)[0], 1)

            def plus_b3(c, tiles=BOTH):
                dve.wait_ge(*o_step(c, tiles, 1))
                nc.vector.tensor_tensor(o[:, tiles, :], o3[:, tiles, :], rows_of(b3_bc, tiles),
                                        ALU.add).then_inc(o_step(c, tiles, 2)[0], 1)

            def statistics_o(c, tiles=BOTH):
                dve.wait_ge(*o_step(c, tiles, 2))
                for t in range(tiles.start, tiles.stop):
                    last = nc.vector.bn_stats(st4[:, t, :], o[:, t, :])
                last.then_inc(o_step(c, tiles, 3)[0], 1)

            def aggregate_o(c, tiles=BOTH):
                dve.wait_ge(*o_step(c, tiles, 3))
                if not (c.known and c.n == 0):
                    dve.wait_ge(ln_rstd, c.upto(2, -1))
                dve.sem_inc(dve_held, 1)
                for t in range(tiles.start, tiles.stop):
                    last = nc.vector.bn_aggr(mv4[:, t, :], st4[:, t, :])
                last.then_inc(o_step(c, tiles, 4)[0], 1)

            def centre_o(c, tiles=BOTH):
                dve.wait_ge(*o_step(c, tiles, 4))
                for t in range(tiles.start, tiles.stop):
                    last = nc.vector.scalar_tensor_tensor(a4[:, t, :], o[:, t, :], mv4[:, t, 0:1], w4_bc[:, :],
                                                          ALU.subtract, ALU.mult)
                last.then_inc(x1_step(c, tiles, 1)[0], 1)

            def add_residual(c, tiles=BOTH):
                dve.wait_ge(*x1_step(c, tiles, 1))
                dve.wait_ge(*rstd_step(c, tiles, 0))
                dve.wait_ge(xb_done, c.upto(1, 1))
                for t in range(tiles.start, tiles.stop):
                    last = nc.vector.scalar_tensor_tensor(x1[c.parity][:, t, :], a4[:, t, :], r4[:, t:t + 1],
                                                          xb[:, t, :], ALU.mult, ALU.add)
                last.then_inc(x1_step(c, tiles, 2)[0], 1)

            def statistics_x1(c, tiles=BOTH):
                dve.wait_ge(*x1_step(c, tiles, 2))
                for t in range(tiles.start, tiles.stop):
                    last = nc.vector.bn_stats(st5[:, t, :], x1[c.parity][:, t, :])
                last.then_inc(x1_step(c, tiles, 3)[0], 1)

            def aggregate_x1(c, tiles=BOTH):
                dve.wait_ge(*x1_step(c, tiles, 3))
                dve.sem_inc(dve_held, 1)
                for t in range(tiles.start, tiles.stop):
                    last = nc.vector.bn_aggr(mv5[:, t, :], st5[:, t, :])
                last.then_inc(x1_step(c, tiles, 4)[0], 1)

            def normalise_x1(c, tiles=BOTH):
                dve.wait_ge(*x1_step(c, tiles, 4))
                dve.wait_ge(*rstd_step(c, tiles, 1))
                if not (c.known and c.n == 0):
                    dve.wait_ge(y_transposed, c.upto(1, 0))
                for t in range(tiles.start, tiles.stop):
                    last = nc.vector.tensor_scalar(y[:, t, :], x1[c.parity][:, t, :], mv5[:, t, 0:1], r5[:, t:t + 1],
                                                   ALU.subtract, ALU.mult)
                if tiles != AHEAD_TILE:
                    last.then_inc(y_done, 1)

            def token_difference(c):
                dve.wait_ge(y_evac, c.upto(1, 1))
                nc.vector.tensor_tensor(dy[:, :], y_t[:, 1:1 + SQ], y_t[:, 0:SQ], ALU.subtract).then_inc(dy_done, 1)

            def mix(c):
                dve.wait_ge(dy_done, c.upto(1, 1))
                if not (c.known and c.n == 0):
                    dve.wait_ge(rk_done, c.upto(1, 0))
                nc.vector.scalar_tensor_tensor(mixed_k[:, :], dy[:, :], column(MUK), y_t[:, 0:SQ], ALU.mult,
                                               ALU.add).then_inc(mixed, 1)
                nc.vector.scalar_tensor_tensor(mixed_r[:, :], dy[:, :], column(MUR), y_t[:, 0:SQ], ALU.mult,
                                               ALU.add).then_inc(mixed, 1)

            def gated_value(c):
                dve.wait_ge(kv_done, c.upto(1, 1))
                nc.vector.scalar_tensor_tensor(gated[:, :, :].rearrange("p t d -> p (t d)"),
                                               gate[:, :, :].rearrange("p t d -> p (t d)"), 1.0, m_ps[:, 0:SQ],
                                               ALU.add, ALU.mult).then_inc(gated_done, 1)

            def final(c):
                dve.wait_ge(gated_done, c.upto(1, 1))
                if not (c.known and c.n < 2):
                    dve.wait_ge(stored[c.parity], c.shift(-2).loads(16))
                nc.vector.scalar_tensor_tensor(result[c.parity][:, :, :], gated[:, :, :], column(TGFH),
                                               x1[c.parity][:, :, :], ALU.mult, ALU.add).then_inc(result_done, 1)

            def iteration(b):
                nxt, prev, old, new = b.shift(1), b.shift(-1), b.shift(-2), b.shift(2)

                if b.known and b.n == -AHEAD:
                    dve.wait_ge(pool_consts, 4)
                if b.known and b.n == -1:
                    combine_first()
                    query_and_key_constants()
                    statistics(new, range(0, 2))
                    normalise_x(nxt)
                    statistics(new, range(2, 4))
                    normalise_first(0)
                    normalise_first(1)
                    high_queries(nxt)
                    low_queries(nxt)
                    low_keys(nxt, 0)
                    low_keys(nxt, 1)
                    statistics(new, range(4, 9))
                    low_keys(nxt, 2)
                    low_keys(nxt, 3)
                    statistics(new, range(9, KT))
                    return
                if b.known and b.n == 1:
                    gate_constants()

                def do(step, batch, *rest):
                    if batch.exists():
                        step(batch, *rest)

                if b.known and b.n == B:
                    times_w3(prev, AHEAD_TILE)
                    plus_b3(prev, AHEAD_TILE)
                    statistics_o(prev, AHEAD_TILE)
                    aggregate_o(prev, AHEAD_TILE)
                    normalise_x1(old)
                    invert_sums(prev, 1)
                    centre_o(prev, AHEAD_TILE)
                    add_residual(prev, AHEAD_TILE)
                    token_difference(old)
                    statistics_x1(prev, AHEAD_TILE)
                    mix(old)
                    aggregate_x1(prev, AHEAD_TILE)
                    times_w3(prev, LAST_TILE)
                    plus_b3(prev, LAST_TILE)
                    statistics_o(prev, LAST_TILE)
                    aggregate_o(prev, LAST_TILE)
                    centre_o(prev, LAST_TILE)
                    normalise_x1(prev, AHEAD_TILE)
                    add_residual(prev, LAST_TILE)
                    statistics_x1(prev, LAST_TILE)
                    aggregate_x1(prev, LAST_TILE)
                    gated_value(old)
                    final(old)
                    return
                if b.known and b.n == B + 1:
                    normalise_x1(old, LAST_TILE)
                    token_difference(old)
                    mix(old)
                    gated_value(old)
                    final(old)
                    return

                do(normalise_x1, old)
                do(statistics, new, range(0, 3))
                do(invert_sums, prev, 1)
                do(maximum, b, 0)
                if b.known and b.n == 0:
                    statistics(new, range(3, 12))
                    invert_sums(b, 0)
                    maximum(b, 1)
                    normalise_x(nxt)
                    high_queries(nxt)
                    low_queries(nxt)
                    low_keys(nxt, 0)
                    statistics(new, range(12, KT))
                    for g in range(1, NG):
                        low_keys(nxt, g)
                    return
                do(token_difference, old)
                do(statistics, new, range(3, 4))
                do(mix, old)
                do(statistics, new, range(4, 7))
                do(normalise_x, nxt)
                do(times_w3, prev)
                do(statistics, new, range(7, 8))
                do(plus_b3, prev)
                do(statistics, new, range(8, 9))
                do(statistics_o, prev)
                do(invert_sums, b, 0)
                do(statistics, new, range(9, 12))
                do(aggregate_o, prev)
                do(maximum, b, 1)
                do(gated_value, old)
                do(centre_o, prev)
                do(final, old)
                do(add_residual, prev)
                do(high_queries, nxt)
                do(statistics_x1, prev)
                do(low_queries, nxt)
                do(low_keys, nxt, 0)
                do(statistics, new, range(12, KT))
                do(aggregate_x1, prev)
                do(low_keys, nxt, 1)
                do(low_keys, nxt, 2)
                do(low_keys, nxt, 3)

            run_pipeline(dve, iteration)


_INS = ["x", "ctx_1024", "g_xattn", "g_ffn", "L0_xattn_inv_scale_factor", "L0_xattn_ln1_w", "L0_xattn_ln1_b",
        "L0_xattn_ln2_w", "L0_xattn_ln2_b", "L0_xattn_ln3_w", "L0_xattn_ln3_b", "L0_xattn_ln4_w", "L0_xattn_ln4_b",
        "L0_ffn_W_r", "L0_ffn_W_k", "L0_ffn_W_v", "L0_ffn_mu_r", "L0_ffn_mu_k"]


def kernel(**inputs):
    import numpy as _np
    import concourse.bacc as _bacc
    from concourse import mybir as _mybir
    from concourse.bass_utils import run_bass_kernel_spmd as _run

    nc = _bacc.Bacc("TRN2", target_bir_lowering=False, num_devices=1)
    arrays, args = {}, []
    for name in _INS:
        a = _np.ascontiguousarray(inputs[name])
        arrays[f"in_{name}"] = a
        args.append(nc.dram_tensor(f"in_{name}", a.shape, _mybir.dt.from_np(a.dtype), kind="ExternalInput").ap())
    out = nc.dram_tensor("out_x", (B, SQ, D), _mybir.dt.float32, kind="ExternalOutput").ap()
    build(nc, *args, out)
    r = _run(nc, [arrays], core_ids=[0])
    return r.results[0]["out_x"]
```
